# Optimizing a Trainium2 kernel written in Bass

```python
import numpy as np
import jax
import jax.numpy as jnp

def _softmax(x, axis=-1):
    return jax.nn.softmax(x, axis=axis)

def _gelu(x):
    return jax.nn.gelu(x, approximate=True)

def _silu(x):
    return jax.nn.silu(x)

def _sigmoid(x):
    return jax.nn.sigmoid(x)

def _layernorm(x, axis=-1, eps=1e-05):
    m = jnp.mean(x, axis=axis, keepdims=True)
    v = jnp.var(x, axis=axis, keepdims=True)
    return (x - m) / jnp.sqrt(v + eps)

def _scatter_add(tgt, idx, src, axis=0):
    return tgt.at[idx].add(src)

def _segment_sum(src, seg, n):
    return jax.ops.segment_sum(src, seg, n)
kernel_name = 'mk_xattn_seq_d1_seqx_r8_8bf6b4'

def setup_inputs(seed: int=0):
    np.random.seed(seed)
    _w = jnp.asarray

    def _rec_inputs():
        import jax
        import jax.numpy as jnp
        _rk = jax.random.key(seed)
        x = -0.0003929 + 0.9999 * jax.random.normal(jax.random.fold_in(_rk, 1), (8, 256, 256), jnp.float32)
        _lenS = 256 - jax.random.randint(jax.random.fold_in(_rk, 7), (8,), 0, max(1, 256 // 4) + 1, jnp.int32)
        _lenS2 = 1601 - jax.random.randint(jax.random.fold_in(_rk, 8), (8,), 0, max(1, 1601 // 4) + 1, jnp.int32)
        _ctx_2048P = jax.random.normal(jax.random.fold_in(_rk, 11), (8, 16, 256), jnp.float32)
        _ctx_2048c = jax.random.dirichlet(jax.random.fold_in(_rk, 511), 0.3 * jnp.ones((16,), jnp.float32), (8, 1601))
        _ctx_2048t = jnp.einsum('bsk,bkd->bsd', _ctx_2048c, _ctx_2048P)
        _ctx_2048t = _ctx_2048t * jax.lax.rsqrt(jnp.mean(jnp.square(_ctx_2048t)) + 1e-12) * 0.953939
        ctx_2048 = -8.57375e-05 + 0.999917 * (_ctx_2048t + 0.3 * jax.random.normal(jax.random.fold_in(_rk, 611), (8, 1601, 256), jnp.float32))
        _validS = jnp.arange(256)[None, :] < _lenS[:, None]
        _validS2 = jnp.arange(1601)[None, :] < _lenS2[:, None]
        _causal = jnp.tril(jnp.ones((256, 256), dtype=bool))
        mask_BxS2_bf1 = jnp.ones((8, 1601), dtype=bool)
        return (x, ctx_2048, mask_BxS2_bf1)
    x, ctx_2048, mask_BxS2_bf1 = _rec_inputs()

    def _L0_xattn_setup():
        import jax, jax.numpy as jnp
        import numpy as np
        HIDDEN = 256
        HEADS = 16
        HEAD_DIM = HIDDEN // HEADS
        LN_EPS = 1e-05
        GATE_INIT = 0.5

        def _layer_norm(x, gamma, beta):
            mu = jnp.mean(x, axis=-1, keepdims=True)
            var = jnp.mean(jnp.square(x - mu), axis=-1, keepdims=True)
            return (x - mu) * jax.lax.rsqrt(var + LN_EPS) * gamma + beta
        key = jax.random.key(seed)
        ks = jax.random.split(key, 8)
        B, T_TEXT, T_AUDIO = (4, 256, 1500)
        s = 0.02
        return {'hidden_states': jax.random.normal(ks[0], (B, T_TEXT, HIDDEN), jnp.float32), 'audio_kv': jax.random.normal(ks[1], (B, T_AUDIO, HIDDEN), jnp.float32), 'audio_attention_mask': jnp.ones((B, T_AUDIO), dtype=bool), 'Wq': jax.random.normal(ks[2], (HIDDEN, HIDDEN), jnp.float32) * s, 'Wk': jax.random.normal(ks[3], (HIDDEN, HIDDEN), jnp.float32) * s, 'Wv': jax.random.normal(ks[4], (HIDDEN, HIDDEN), jnp.float32) * s, 'Wo': jax.random.normal(ks[5], (HIDDEN, HIDDEN), jnp.float32) * s, 'ln_gamma': jnp.ones((HIDDEN,), jnp.float32), 'ln_beta': jnp.zeros((HIDDEN,), jnp.float32), 'gate': jnp.array([GATE_INIT], jnp.float32)}
    _L0_xattn_all = _L0_xattn_setup()
    _L0_xattn_in = {k: v for k, v in _L0_xattn_all.items() if k in ('Wq', 'Wk', 'Wv', 'Wo', 'ln_gamma', 'ln_beta', 'gate')}
    del _L0_xattn_all
    return {'x': x, 'ctx_2048': ctx_2048, 'mask_BxS2_bf1': mask_BxS2_bf1, 'L0_xattn_Wq': _L0_xattn_in['Wq'], 'L0_xattn_Wk': _L0_xattn_in['Wk'], 'L0_xattn_Wv': _L0_xattn_in['Wv'], 'L0_xattn_Wo': _L0_xattn_in['Wo'], 'L0_xattn_ln_gamma': _L0_xattn_in['ln_gamma'], 'L0_xattn_ln_beta': _L0_xattn_in['ln_beta'], 'L0_xattn_gate': _L0_xattn_in['gate']}

def reference(x, ctx_2048, mask_BxS2_bf1, L0_xattn_Wq, L0_xattn_Wk, L0_xattn_Wv, L0_xattn_Wo, L0_xattn_ln_gamma, L0_xattn_ln_beta, L0_xattn_gate):
    import jax
    import jax.numpy as jnp

    def _L0_xattn_ref(hidden_states, audio_kv, audio_attention_mask, Wq, Wk, Wv, Wo, ln_gamma, ln_beta, gate):
        import jax, jax.numpy as jnp
        import numpy as np
        HIDDEN = 256
        HEADS = 16
        HEAD_DIM = HIDDEN // HEADS
        LN_EPS = 1e-05
        GATE_INIT = 0.5

        def _layer_norm(x, gamma, beta):
            mu = jnp.mean(x, axis=-1, keepdims=True)
            var = jnp.mean(jnp.square(x - mu), axis=-1, keepdims=True)
            return (x - mu) * jax.lax.rsqrt(var + LN_EPS) * gamma + beta
        B, Tt, D = hidden_states.shape
        Ta = audio_kv.shape[1]
        scale = HEAD_DIM ** (-0.5)
        a = _layer_norm(audio_kv, ln_gamma, ln_beta)
        Q = (hidden_states @ Wq.T).reshape(B, Tt, HEADS, HEAD_DIM).transpose(0, 2, 1, 3)
        K = (a @ Wk.T).reshape(B, Ta, HEADS, HEAD_DIM).transpose(0, 2, 1, 3)
        V = (a @ Wv.T).reshape(B, Ta, HEADS, HEAD_DIM).transpose(0, 2, 1, 3)
        scores = jnp.einsum('bhtd,bhsd->bhts', Q, K) * scale
        mask = audio_attention_mask[:, None, None, :]
        scores = jnp.where(mask, scores, jnp.float32(-jnp.inf))
        attn = jax.nn.softmax(scores, axis=-1)
        out = jnp.einsum('bhts,bhsd->bhtd', attn, V)
        out = out.transpose(0, 2, 1, 3).reshape(B, Tt, D)
        out = out @ Wo.T
        return hidden_states + jnp.tanh(gate) * out
    x = _L0_xattn_ref(x, ctx_2048, mask_BxS2_bf1, L0_xattn_Wq, L0_xattn_Wk, L0_xattn_Wv, L0_xattn_Wo, L0_xattn_ln_gamma, L0_xattn_ln_beta, L0_xattn_gate)
    return x

_drawn_inputs = setup_inputs


def setup_inputs(seed=0):
    import zlib

    import numpy as np

    out = dict(_drawn_inputs(seed))
    spreads = {'L0_xattn_ln_gamma': (1.0, 0.6), 'L0_xattn_ln_beta': (0.0, 0.8)}
    factors = {'L0_xattn_Wq': 8.0, 'L0_xattn_Wk': 8.0}
    for name, (base, spread) in spreads.items():
        noise = np.random.default_rng([zlib.crc32(name.encode()), seed]).standard_normal(out[name].shape)
        drawn = base * np.exp(spread * noise) if base else spread * noise
        out[name] = jnp.asarray(drawn.astype(out[name].dtype))
    for name, factor in factors.items():
        out[name] = (out[name] * factor).astype(out[name].dtype)
    return out
```

```python
import struct
from contextlib import ExitStack

import numpy as np

import concourse.bass as bass
from concourse import mybir

ALU = mybir.AluOpType
ACT = mybir.ActivationFunctionType
AX = mybir.AxisListType
F32 = mybir.dt.float32
BF16 = mybir.dt.bfloat16
U8 = mybir.dt.uint8

P = 128
B, T, S, D = 8, 256, 1601, 256
HEADS, HD = 16, 16
SCALE = HD ** -0.5
EPS = 1e-5
MASKED = -1e30

TC = T // P
DC = D // P
SC = -(-S // P)
SPAD = SC * P
SLAST = S - (SC - 1) * P
QUAD = 4
QUADS = HEADS // QUAD
STEPS = QUADS * SC
PARTS = 3
ROWS = 6 * HD
MASK_ROW = ROWS
MAX_ROWS = ROWS + 1
ALL_ROWS = ROWS + 1 + PARTS
K_PARTS = (0, 0, 0, 1, 1, 2)
Q_PARTS = (0, 1, 2, 0, 1, 0)
PIECES = 4
CUTS = [0, 401, 801, 1201, S]
FINDS = QUAD * TC * PIECES
PROBS = 4
RESID = 4
KHALF = 2

FINDS_AT = [4] * 8 + [0] * 5
assert sum(FINDS_AT) == FINDS and len(FINDS_AT) == SC

UNITS = sorted(
    [(0, "V", 6, 0), (1, "O", 3, -1), (3, "A", 0, -1), (5, "F", 0, -1)]
    + [(SC * (q + 1) + 1, "O", q, 0) for q in range(QUADS - 1)]
    + [(SC * q + 9 + u, "M", 2 * ((q + 1) % QUADS) + u, (q + 1) // QUADS) for q in range(QUADS) for u in range(2)]
    + [(4, "QT", 0, 1), (6, "QP", 0, 1)]
    + [(s, "XT", n, 1) for n, s in enumerate((12, 13, 15, 16, 18, 19, 20))]
    + [(s, "K", n, 1) for n, s in enumerate((21, 24, 25, 26, 28, 29, 30, 31))]
    + [(SC * (QUADS - 1) + 2 * n + 2, "V", n, 1) for n in range(6)],
    key=lambda u: u[0],
)
PER = {k: sum(u[1] == k for u in UNITS) for k in {u[1] for u in UNITS}}
STATS_AT = {1 + n: [2 * n + i for i in range(2) if 2 * n + i < SC] for n in range((SC + 1) // 2)}
NORM_STEP = 1 + len(STATS_AT)


def units_of(b):
    return [u for u in UNITS if 0 <= b + u[3] < B]


def xattn_kernel(nc, x, ctx, mask, wq, wk, wv, wo, gamma, beta, gate, out):
    with ExitStack() as stack:
        def sb(name, shape, dt=F32):
            return stack.enter_context(nc.sbuf_tensor(name, shape, dt))

        def ps(name, shape, dt=F32):
            return stack.enter_context(nc.psum_tensor(name, shape, dt))

        def sem(name):
            return stack.enter_context(nc.semaphore(name))

        k_scratch = nc.dram_tensor("k_scratch", (PARTS, HEADS * HD, S), BF16, kind="Internal").ap()
        q_scratch = nc.dram_tensor("q_scratch", (PARTS, HEADS * HD, T), BF16, kind="Internal").ap()
        bias_scratch = nc.dram_tensor("bias_scratch", (B, SPAD), BF16, kind="Internal").ap()

        scores = ps("scores", [P, 2, QUAD * T])
        found = ps("found", [P, 2, 512])
        mixed = ps("mixed", [P, 512])
        side = ps("side", [P, 512])

        k_rows = sb("k_rows", [P, HEADS, SPAD], BF16)
        q_rows = sb("q_rows", [P, HEADS, T], BF16)
        v_rows = sb("v_rows", [P, SC, HEADS, HD + 1])
        probs = sb("probs", [P, PROBS, QUAD * T])
        audio = sb("audio", [P, SC, D])
        audio_t = sb("audio_t", [P, DC, S])
        k_parts = sb("k_parts", [P, KHALF, PARTS, S], BF16)
        k_rest = sb("k_rest", [P, RESID, 512])
        text = sb("text", [P, TC, D])
        text_t = sb("text_t", [P, DC, T])
        q_parts = sb("q_parts", [P, PARTS, KHALF * T], BF16)
        q_rest = sb("q_rest", [P, KHALF * T])
        w_in = sb("w_in", [P, 4, DC, D])
        w_t = sb("w_t", [P, 4, DC, D])
        ident = sb("ident", [P, P])
        ident_bf = sb("ident_bf", [P, P], BF16)
        gamma_c = sb("gamma_c", [P, DC])
        beta_c = sb("beta_c", [P, DC])
        gate_c = sb("gate_c", [P, 1])
        tanh_gate = sb("tanh_gate", [P, 1])
        mask_u8 = sb("mask_u8", [B, S], U8)
        bias_bf = sb("bias_bf", [B, SPAD], BF16)
        mask_tiles = sb("mask_tiles", [B * SC, P], U8)
        mask_f = sb("mask_f", [B * SC, P])
        mask_t = sb("mask_t", [P, B * SC])
        mask_c = sb("mask_c", [P, SC])
        bn = sb("bn", [P, SC, 6])
        mean_var = sb("mean_var", [P, SC, 2])
        var_eps = sb("var_eps", [P, SC])
        minus_half = sb("minus_half", [P, SC])
        rstd0 = sb("rstd0", [P, SC])
        newton = sb("newton", [P, 3, SC])
        rstd = sb("rstd", [P, SC])
        piece_max = sb("piece_max", [P, QUAD * TC, PIECES])
        neg_max = sb("neg_max", [P, QUAD * TC])
        neg_rest = sb("neg_rest", [P, QUAD * TC])
        neg_parts = sb("neg_parts", [P, QUAD * TC, 1 + PARTS], BF16)
        mixed_sb = sb("mixed_sb", [P, T])
        inv_sum = sb("inv_sum", [P, TC, QUAD])
        attn = sb("attn", [P, TC, D])
        attn_t = sb("attn_t", [P, DC * TC, P])
        residual = sb("residual", [P, TC, D])
        result = sb("result", [P, TC, D])

        full = {k: sem(f"full_{k}") for k in [*PER, "W", "MT"]}
        taken = {k: sem(f"taken_{k}") for k in [*PER, "W", "MT"]}
        scores_full = sem("scores_full")
        probs_ready = sem("probs_ready")
        mixed_done = sem("mixed_done")
        mixed_taken = sem("mixed_taken")
        found_full = sem("found_full")
        found_taken = sem("found_taken")
        max_chain = sem("max_chain")
        max_parts = sem("max_parts")
        inverted = sem("inverted")
        k_high = sem("k_high")
        q_high = sem("q_high")
        k_mid = sem("k_mid")
        q_mid = sem("q_mid")
        k_split = sem("k_split")
        q_split = sem("q_split")
        stats = sem("stats")
        moments = sem("moments")
        eps_added = sem("eps_added")
        powered = sem("powered")
        newton_chain = sem("newton_chain")
        rstd_ready = sem("rstd_ready")
        normed = sem("normed")
        mask_col = sem("mask_col")
        v_mask = sem("v_mask")
        audio_in = sem("audio_in")
        text_in = sem("text_in")
        residual_in = sem("residual_in")
        stored = sem("stored")
        k_stored = [sem(f"k_stored{h}") for h in range(KHALF)]
        q_stored = sem("q_stored")
        quad_in = [sem(f"quad_in{q}") for q in range(QUADS)]
        w_loaded = sem("w_loaded")
        consts_in = sem("consts_in")
        mask_in = sem("mask_in")
        bias_stored = sem("bias_stored")
        ident0 = sem("ident0")
        ident_ready = sem("ident_ready")
        ident_bf_ready = sem("ident_bf_ready")
        tiles_zero = sem("tiles_zero")
        audio_pad = sem("audio_pad")
        bias_ready = sem("bias_ready")
        bias_pad = sem("bias_pad")
        mask_f_ready = sem("mask_f_ready")
        pool_ready = sem("pool_ready")
        ones_ready = sem("ones_ready")
        dve_ready = sem("dve_ready")
        gate_ready = sem("gate_ready")

        passed = sem("passed")

        DMA = 16
        QUAD_DMAS = 13
        AUDIO_DMAS = 4

        def wait(eng, semaphore, value):
            if isinstance(value, int) and value <= 0:
                return
            eng.wait_ge(semaphore, value)

        def own_instruction(eng):
            eng.sem_inc(passed, 1)

        def wait_apart(eng, semaphore, value):
            if isinstance(value, int) and value <= 0:
                return
            eng.wait_ge(semaphore, value)
            if not isinstance(value, int):
                own_instruction(eng)

        def exists(b):
            return not isinstance(b, int) or 0 <= b < B

        def as_int(b):
            return b if isinstance(b, int) else 1

        def run_batches(eng, body):
            body(-1)
            body(0)
            with eng.Fori(1, B - 1) as b:
                body(b)
            body(B - 1)
            body(B)

        def side_units(b, k):
            return [(u[1], u[2], b + u[3]) for u in units_of(as_int(b)) if u[0] == k]

        block = stack.enter_context(nc.Block())

        def load_audio(sp, b):
            wait_apart(sp, full["XT"], PER["XT"] * b)
            if isinstance(b, int) and b == 0:
                sp.wait_ge(audio_pad, 1)
            for c in range(0, SC - 1, 4):
                sp.dma_start(audio[:, c:c + 4, :],
                             ctx[b, c * P:(c + 4) * P, :].rearrange("(c p) d -> p c d", p=P))\
                  .then_inc(audio_in, DMA)
            sp.dma_start(audio[0:SLAST, SC - 1, :], ctx[b, (SC - 1) * P:S, :]).then_inc(audio_in, DMA)

        def load_text(sp, b):
            wait_apart(sp, full["QT"], b)
            sp.dma_start(text[:, :, :], x[b].rearrange("(c p) d -> p c d", p=P)).then_inc(text_in, DMA)

        @block.sync
        def _(sp):
            for n, w in enumerate((wk, wv, wq, wo)):
                sp.dma_start(w_in[:, n], w.rearrange("(c p) d -> p c d", p=P)).then_inc(w_loaded, DMA)
            load_audio(sp, 0)
            load_text(sp, 0)
            sp.dma_start(mask_u8[:, :], mask).then_inc(mask_in, DMA)
            sp.wait_ge(tiles_zero, 1)
            whole = (SC - 1) * P
            for b in range(B):
                sp.dma_start(mask_tiles[b * (SC - 1):(b + 1) * (SC - 1), :],
                             mask[b, 0:whole].rearrange("(c p) -> c p", p=P)).then_inc(mask_in, DMA)
            sp.dma_start(mask_tiles[B * (SC - 1):B * SC, 0:SLAST], mask[:, whole:S]).then_inc(mask_in, DMA)
            sp.wait_ge(bias_ready, 1)
            sp.dma_start(bias_scratch, bias_bf[:, :]).then_inc(bias_stored, DMA)
            sp.wait_ge(bias_stored, DMA)

            def load_quad(b, q):
                wait_apart(sp, scores_full, STEPS * (b - 1) + SC * (q + 1))
                if as_int(b) == 0:
                    sp.wait_ge(ones_ready, q + 1)
                slots = slice(QUAD * q, QUAD * (q + 1))
                lines = slice(QUAD * HD * q, QUAD * HD * (q + 1))
                for g in range(6):
                    sp.dma_start(k_rows[HD * g:HD * (g + 1), slots, 0:S],
                                 k_scratch[K_PARTS[g], lines, :].rearrange("(h d) s -> d h s", d=HD))\
                      .then_inc(quad_in[q], DMA)
                for g in range(6):
                    sp.dma_start(q_rows[HD * g:HD * (g + 1), slots, :],
                                 q_scratch[Q_PARTS[g], lines, :].rearrange("(h d) t -> d h t", d=HD))\
                      .then_inc(quad_in[q], DMA)
                sp.dma_start(k_rows[MASK_ROW:MASK_ROW + 1, slots, :],
                             bias_scratch[bass.ds(b, 1), :].unsqueeze(1).broadcast_to([1, QUAD, SPAD]))\
                  .then_inc(quad_in[q], DMA)

            def body(b):
                if exists(b):
                    load_quad(b, QUADS - 1)
                if exists(b + 1) and as_int(b) >= 0:
                    load_audio(sp, b + 1)
                    load_text(sp, b + 1)
                if exists(b - 1):
                    wait_apart(sp, taken["F"], b)
                    sp.dma_start(out[b - 1].rearrange("(c p) d -> p c d", p=P), result[:, :, :])\
                      .then_inc(stored, DMA)
                if exists(b):
                    wait_apart(sp, taken["F"], b)
                    sp.dma_start(residual[:, :, :], x[b].rearrange("(c p) d -> p c d", p=P))\
                      .then_inc(residual_in, DMA)
                if exists(b + 1):
                    n = b + 1
                    wait_apart(sp, q_split, n + 1)
                    for q in range(QUADS):
                        wait_apart(sp, quad_in[q], DMA * QUAD_DMAS * n)
                    for half in range(KHALF):
                        sp.dma_start(q_scratch[:, P * half:P * (half + 1), :].rearrange("a p t -> p a t"),
                                     q_parts[:, :, T * half:T * (half + 1)]).then_inc(q_stored, DMA)
                    for half in range(KHALF):
                        wait_apart(sp, k_split, PER["K"] * n + PIECES * (half + 1))
                        sp.dma_start(k_scratch[:, P * half:P * (half + 1), :].rearrange("a p s -> p a s"),
                                     k_parts[:, half]).then_inc(k_stored[half], DMA)
                        if half == 0:
                            wait_apart(sp, q_stored, DMA * KHALF * (n + 1))
                        wait_apart(sp, k_stored[half], DMA * (n + 1))
                        for q in (2 * half, 2 * half + 1):
                            if q < QUADS - 1:
                                load_quad(n, q)

            run_batches(sp, body)
            sp.wait_ge(stored, DMA * B)

        @block.tensor
        def _(pe):
            pe.wait_ge(ident_ready, 1)
            pe.wait_ge(w_loaded, 4 * DMA)
            for n in range(4):
                wait(pe, taken["W"], n)
                for i in range(DC):
                    for o in range(DC):
                        mm = nc.tensor.transpose(side[:, D * i + P * o:D * i + P * (o + 1)],
                                                 w_in[:, n, o, P * i:P * (i + 1)], ident[:, :])
                mm.then_inc(full["W"], 1)
            pe.wait_ge(taken["W"], 4)
            pe.wait_ge(mask_f_ready, 1)
            nc.tensor.transpose(side[:, 0:B * SC], mask_f[:, :], ident[0:B * SC, 0:B * SC])\
                .then_inc(full["MT"], 1)
            pe.wait_ge(ident_bf_ready, 1)
            pe.wait_ge(dve_ready, 1)
            pe.wait_ge(pool_ready, 1)

            def previous(b, n):
                units = units_of(as_int(b))
                if n > 0:
                    u = units[n - 1]
                    return u[1], u[2], b + u[3]
                if as_int(b) == -1:
                    return "MT", 0, 0
                u = units_of(as_int(b) - 1)[-1]
                return u[1], u[2], b - 1 + u[3]

            def free_side(b, n):
                kind, index, batch = previous(b, n)
                pe.wait_ge(taken[kind], PER.get(kind, 1) * batch + index + 1)

            def unit(kind, index, n):
                if kind == "V":
                    chunks = [c for c in (2 * index, 2 * index + 1) if c < SC]
                    for c in chunks:
                        rows = P if c < SC - 1 else SLAST
                        for i in range(DC):
                            mm = nc.tensor.matmul(side[0:rows, D * (c % 2):D * (c % 2 + 1)],
                                                  audio_t[:, i, P * c:P * c + rows], w_t[:, 1, i, :],
                                                  start=(i == 0), stop=(i == DC - 1))
                elif kind == "K":
                    half, piece = divmod(index, PIECES)
                    if index == 0:
                        pe.wait_ge(taken["XT"], PER["XT"] * (n + 1))
                    lo, hi = CUTS[piece], CUTS[piece + 1]
                    for i in range(DC):
                        mm = nc.tensor.matmul(side[:, 0:hi - lo], w_t[:, 0, i, P * half:P * (half + 1)],
                                              audio_t[:, i, lo:hi], start=(i == 0), stop=(i == DC - 1))
                elif kind == "XT":
                    if index < PER["XT"] - 1:
                        group, i = divmod(index, DC)
                        pe.wait_ge(normed, SC * n + 4 * group + 4)
                        for c in range(4):
                            mm = nc.tensor.transpose(side[:, P * c:P * (c + 1)],
                                                     audio[:, 4 * group + c, P * i:P * (i + 1)], ident[:, :])
                    else:
                        pe.wait_ge(normed, SC * n + SC)
                        for i in range(DC):
                            mm = nc.tensor.transpose(side[:, P * i:P * i + SLAST],
                                                     audio[0:SLAST, SC - 1, P * i:P * (i + 1)],
                                                     ident[0:SLAST, 0:SLAST])
                elif kind == "QT":
                    pe.wait_ge(text_in, DMA * (n + 1))
                    for i in range(DC):
                        for c in range(TC):
                            mm = nc.tensor.transpose(side[:, T * i + P * c:T * i + P * (c + 1)],
                                                     text[:, c, P * i:P * (i + 1)], ident[:, :])
                elif kind == "QP":
                    for half in range(KHALF):
                        for i in range(DC):
                            mm = nc.tensor.matmul(side[:, T * half:T * (half + 1)],
                                                  w_t[:, 2, i, P * half:P * (half + 1)], text_t[:, i, :],
                                                  start=(i == 0), stop=(i == DC - 1))
                elif kind == "M":
                    q, u = divmod(index, 2)
                    if u == 0:
                        pe.wait_ge(max_parts, QUADS * n + q + 1)
                    for m in range(2 * TC):
                        mm = nc.tensor.matmul(side[MASK_ROW:ALL_ROWS, P * m:P * (m + 1)],
                                              neg_parts[:, 2 * TC * u + m, :], ident_bf[:, :],
                                              start=True, stop=True)
                elif kind == "O":
                    pe.wait_ge(mixed_taken, QUADS * n + index + 1)
                    for c in range(TC):
                        mm = nc.tensor.transpose(side[:, P * c:P * (c + 1)],
                                                 mixed_sb[:, P * c:P * (c + 1)], ident[:, :])
                elif kind == "A":
                    pe.wait_ge(taken["O"], QUADS * (n + 1))
                    for i in range(DC):
                        for c in range(TC):
                            m = TC * i + c
                            mm = nc.tensor.transpose(side[:, P * m:P * (m + 1)],
                                                     attn[:, c, P * i:P * (i + 1)], ident[:, :])
                else:
                    for c in range(TC):
                        for i in range(DC):
                            mm = nc.tensor.matmul(side[:, D * c:D * (c + 1)], attn_t[:, TC * i + c, :],
                                                  w_t[:, 3, i, :], start=(i == 0), stop=(i == DC - 1))
                mm.then_inc(full[kind], 1)

            def score(b, k, heads):
                q, c = divmod(k, SC)
                for j in heads:
                    h = QUAD * q + j
                    mm = nc.tensor.matmul(scores[:, k % 2, T * j:T * (j + 1)],
                                          k_rows[0:ALL_ROWS, h, P * c:P * (c + 1)],
                                          q_rows[0:ALL_ROWS, h, :], start=True, stop=True)
                if heads[-1] == QUAD - 1:
                    mm.then_inc(scores_full, 1)

            def find(b, q, n):
                quad = QUADS * b + q
                if n == 0:
                    pe.wait_ge(quad_in[q], DMA * QUAD_DMAS * (b + 1))
                wait(pe, found_taken, FINDS * quad + n - 1)
                j, c, piece = n // (TC * PIECES), n // PIECES % TC, n % PIECES
                h = QUAD * q + j
                lo, hi = CUTS[piece], CUTS[piece + 1]
                nc.tensor.matmul(found[:, n % 2, 0:hi - lo], q_rows[0:MAX_ROWS, h, P * c:P * (c + 1)],
                                 k_rows[0:MAX_ROWS, h, lo:hi], start=True, stop=True)\
                    .then_inc(found_full, 1)

            def mix(b, k):
                q, c = divmod(k, SC)
                pe.wait_ge(probs_ready, STEPS * b + k + 1)
                if c == 0:
                    wait(pe, mixed_taken, QUADS * b + q)
                if q == 0 and c % 2 == 0:
                    pe.wait_ge(taken["V"], PER["V"] * b + c // 2 + 1)
                    pe.wait_ge(v_mask, PER["V"] * b + c // 2 + 1)
                for j in range(QUAD):
                    mm = nc.tensor.matmul(mixed[32 * j:32 * j + HD + 1, 0:T], v_rows[:, c, QUAD * q + j, :],
                                          probs[:, k % PROBS, T * j:T * (j + 1)],
                                          start=(c == 0), stop=(c == SC - 1))
                mm.then_inc(mixed_done, 1)

            def body(b):
                n_unit = 0
                for k in range(STEPS):
                    q, c = divmod(k, SC)
                    nb, nq = (b, q + 1) if q < QUADS - 1 else (b + 1, 0)
                    finds = iter([])
                    if exists(nb) and (nq == 0 or exists(b)):
                        first = sum(FINDS_AT[:c])
                        finds = iter(range(first, first + FINDS_AT[c]))

                    def find_next(count=1):
                        for _ in range(count):
                            n = next(finds, None)
                            if n is not None:
                                find(nb, nq, n)

                    if exists(b):
                        wait(pe, probs_ready, STEPS * b + k - 1)
                        if c == 0:
                            pe.wait_ge(taken["M"], 2 * (QUADS * b + q + 1))
                        score(b, k, [0, 1])
                    find_next()
                    if exists(b):
                        score(b, k, [2, 3])
                    find_next()
                    for kind, index, n in side_units(b, k):
                        free_side(b, n_unit)
                        unit(kind, index, n)
                        n_unit += 1
                    find_next()
                    if k > 0 and exists(b):
                        mix(b, k - 1)
                    if k == 0 and exists(b - 1):
                        mix(b - 1, STEPS - 1)
                    find_next(FINDS)

            run_batches(pe, body)

        @block.scalar
        def _(act):
            act.dma_start(gamma_c[:, :], gamma.rearrange("(c p) -> p c", p=P),
                          allow_slow_non_contiguous=True).then_inc(consts_in, DMA)
            act.dma_start(beta_c[:, :], beta.rearrange("(c p) -> p c", p=P),
                          allow_slow_non_contiguous=True).then_inc(consts_in, DMA)
            act.dma_start(gate_c[:, :], gate.partition_broadcast(P)).then_inc(consts_in, DMA)
            act.wait_ge(consts_in, 3 * DMA)
            nc.scalar.activation(tanh_gate[:, :], gate_c[:, :], ACT.Tanh).then_inc(gate_ready, 1)
            act.wait_ge(pool_ready, 1)
            act.wait_ge(dve_ready, 1)

            def take(kind, index, n):
                if kind == "XT":
                    act.wait_ge(full["XT"], PER["XT"] * n + index + 1)
                    if index < PER["XT"] - 1:
                        group, i = divmod(index, DC)
                        spans = [(i, 4 * P * group, 4 * P, 0)]
                    else:
                        spans = [(i, P * (SC - 1), SLAST, P * i) for i in range(DC)]
                    for i, to, width, frm in spans:
                        last = nc.scalar.activation(audio_t[:, i, to:to + width], side[:, frm:frm + width],
                                                    ACT.Identity, bias=beta_c[:, i:i + 1],
                                                    scale=gamma_c[:, i:i + 1])
                    last.then_inc(taken["XT"], 1)
                elif kind == "QT":
                    act.wait_ge(full["QT"], n + 1)
                    nc.scalar.activation(text_t[:, :, :].rearrange("p i t -> p (i t)"), side[:, 0:DC * T],
                                         ACT.Copy).then_inc(taken["QT"], 1)
                elif kind == "QP":
                    act.wait_ge(full["QP"], n + 1)
                    wait(act, q_stored, DMA * KHALF * n)
                    nc.scalar.activation(q_parts[:, 0, :], side[:, :], ACT.Copy, scale=SCALE)\
                        .then_inc(q_high, 1)
                elif kind == "K":
                    half, piece = divmod(index, PIECES)
                    act.wait_ge(full["K"], PER["K"] * n + index + 1)
                    if piece == 0:
                        wait(act, k_stored[half], DMA * n)
                    lo, hi = CUTS[piece], CUTS[piece + 1]
                    nc.scalar.activation(k_parts[:, half, 0, lo:hi], side[:, 0:hi - lo], ACT.Copy)\
                        .then_inc(k_high, 1)
                elif kind == "V":
                    act.wait_ge(full["V"], PER["V"] * n + index + 1)
                    if index == 0:
                        act.wait_ge(mask_col, n + 1)
                    chunks = [c for c in (2 * index, 2 * index + 1) if c < SC]
                    wait(act, mixed_done, STEPS * (n - 1) + SC * (QUADS - 1) + chunks[-1] + 1)
                    for c in chunks:
                        rows = P if c < SC - 1 else SLAST
                        last = nc.scalar.activation(
                            v_rows[0:rows, c, :, 0:HD],
                            side[0:rows, D * (c % 2):D * (c % 2 + 1)].rearrange("p (h d) -> p h d", d=HD),
                            ACT.Copy, scale=mask_c[0:rows, c:c + 1])
                    last.then_inc(taken["V"], 1)
                elif kind == "M":
                    q, u = divmod(index, 2)
                    act.wait_ge(full["M"], PER["M"] * n + index + 1)
                    h = QUAD * q + 2 * u
                    nc.scalar.activation(q_rows[MASK_ROW:ALL_ROWS, h:h + 2, :].rearrange("p h t -> p (h t)"),
                                         side[MASK_ROW:ALL_ROWS, :], ACT.Copy).then_inc(taken["M"], 1)
                elif kind == "A":
                    act.wait_ge(full["A"], n + 1)
                    nc.scalar.activation(attn_t[:, :, :].rearrange("p m t -> p (m t)"), side[:, :], ACT.Copy)\
                        .then_inc(taken["A"], 1)

            def body(b):
                for k in range(STEPS):
                    if exists(b):
                        act.wait_ge(scores_full, STEPS * b + k + 1)
                        wait(act, mixed_done, STEPS * b + k - PROBS + 1)
                        nc.scalar.activation(probs[:, k % PROBS, :], scores[:, k % 2, :], ACT.Exp)\
                            .then_inc(probs_ready, 1)
                    for kind, index, n in side_units(b, k):
                        take(kind, index, n)

            run_batches(act, body)

        @block.vector
        def _(dve):
            nc.vector.memset(mask_tiles[:, :], 0).then_inc(tiles_zero, 1)
            nc.vector.memset(bias_bf[:, :], MASKED).then_inc(bias_pad, 1)
            nc.vector.memset(audio[64:P, SC - 1, :], 0.0).then_inc(audio_pad, 1)
            nc.vector.memset(mean_var[:, :, :], 1.0)
            nc.vector.memset(minus_half[:, :], -0.5)
            nc.vector.memset(q_rows[MASK_ROW:ALL_ROWS, :, :], 1.0)
            nc.vector.memset(neg_parts[:, :, :], 1.0)
            nc.vector.memset(v_rows[64:P, SC - 1], 0.0)
            nc.vector.memset(mixed[:, :], 0.0).then_inc(dve_ready, 1)
            dve.wait_ge(ident_ready, 1)
            nc.vector.tensor_copy(ident_bf[:, :], ident[:, :]).then_inc(ident_bf_ready, 1)
            dve.wait_ge(mask_in, DMA * (B + 2))
            dve.wait_ge(bias_pad, 1)
            nc.vector.tensor_scalar(bias_bf[:, 0:S], mask_u8[:, :], -1.0, -MASKED, ALU.add, ALU.mult)\
                .then_inc(bias_ready, 1)
            nc.vector.tensor_copy(mask_f[:, :], mask_tiles[:, :]).then_inc(mask_f_ready, 1)
            for n in range(4):
                dve.wait_ge(full["W"], n + 1)
                nc.vector.tensor_copy(w_t[:, n].rearrange("p i o -> p (i o)"), side[:, :]).then_inc(taken["W"], 1)
            dve.wait_ge(full["MT"], 1)
            nc.vector.tensor_copy(mask_t[:, :], side[:, 0:B * SC]).then_inc(taken["MT"], 1)
            dve.wait_ge(gate_ready, 1)

            def search(b, q, n):
                quad = QUADS * b + q
                piece = n % PIECES
                width = CUTS[piece + 1] - CUTS[piece]
                dve.wait_ge(found_full, FINDS * quad + n + 1)
                nc.vector.tensor_reduce(piece_max[:, n // PIECES, piece:piece + 1], found[:, n % 2, 0:width],
                                        AX.X, ALU.max).then_inc(found_taken, 1)

            def split_max(b, q):
                quad = QUADS * b + q
                dve.wait_ge(found_taken, FINDS * (quad + 1))
                nc.vector.tensor_reduce(neg_max[:, :], piece_max[:, :, :], AX.X, ALU.max, negate=True)\
                    .then_inc(max_chain, 1)
                wait(dve, full["M"], 2 * quad)
                dve.wait_ge(max_chain, 4 * quad + 1)
                nc.vector.tensor_copy(neg_parts[:, :, 1], neg_max[:, :]).then_inc(max_chain, 1)
                dve.wait_ge(max_chain, 4 * quad + 2)
                nc.vector.tensor_tensor(neg_rest[:, :], neg_max[:, :], neg_parts[:, :, 1], ALU.subtract)\
                    .then_inc(max_chain, 1)
                dve.wait_ge(max_chain, 4 * quad + 3)
                nc.vector.tensor_copy(neg_parts[:, :, 2], neg_rest[:, :]).then_inc(max_chain, 1)
                dve.wait_ge(max_chain, 4 * quad + 4)
                nc.vector.tensor_tensor(neg_parts[:, :, 3], neg_rest[:, :], neg_parts[:, :, 2], ALU.subtract)\
                    .then_inc(max_parts, 1)

            def take(kind, index, n):
                if kind == "K":
                    dve.wait_ge(k_high, PER["K"] * n + index + 1)
                    wait(dve, k_split, PER["K"] * n + index + 1 - RESID)
                    half, piece = divmod(index, PIECES)
                    lo, hi = CUTS[piece], CUTS[piece + 1]
                    nc.vector.tensor_tensor(k_rest[:, index % RESID, 0:hi - lo], side[:, 0:hi - lo],
                                            k_parts[:, half, 0, lo:hi], ALU.subtract).then_inc(taken["K"], 1)
                elif kind == "QP":
                    dve.wait_ge(q_high, n + 1)
                    nc.vector.scalar_tensor_tensor(q_rest[:, :], side[:, :], SCALE, q_parts[:, 0, :],
                                                   ALU.mult, ALU.subtract).then_inc(taken["QP"], 1)
                elif kind == "O":
                    quad = QUADS * n + index
                    dve.wait_ge(full["O"], quad + 1)
                    sums = side[:, 0:TC * P].rearrange("p (c j e) -> p c j e", c=TC, j=QUAD)
                    nc.vector.reciprocal(inv_sum[:, :, :], sums[:, :, :, HD]).then_inc(inverted, 1)
                    dve.wait_ge(inverted, quad + 1)
                    width = QUAD * HD
                    nc.vector.tensor_tensor(
                        attn[:, :, width * index:width * (index + 1)].rearrange("p c (j d) -> p c j d", j=QUAD),
                        sums[:, :, :, 0:HD],
                        inv_sum[:, :, :].unsqueeze(3).broadcast_to([P, TC, QUAD, HD]),
                        ALU.mult).then_inc(taken["O"], 1)
                elif kind == "F":
                    dve.wait_ge(full["F"], n + 1)
                    dve.wait_ge(residual_in, DMA * (n + 1))
                    wait(dve, stored, DMA * n)
                    nc.vector.scalar_tensor_tensor(
                        result[:, :, :].rearrange("p c d -> p (c d)"), side[:, :], tanh_gate[:, 0:1],
                        residual[:, :, :].rearrange("p c d -> p (c d)"), ALU.mult, ALU.add)\
                        .then_inc(taken["F"], 1)

            def statistics(n, c):
                rows = P if c < SC - 1 else SLAST
                nc.vector.bn_stats(bn[0:rows, c, :], audio[0:rows, c, :]).then_inc(stats, 1)

            def aggregate(n, c):
                rows = P if c < SC - 1 else SLAST
                dve.wait_ge(stats, SC * n + c + 1)
                own_instruction(dve)
                nc.vector.bn_aggr(mean_var[0:rows, c, :], bn[0:rows, c, :]).then_inc(moments, 1)

            def refine(n):
                y, t = rstd0[:, :], [newton[:, i, :] for i in range(3)]
                dve.wait_ge(powered, n + 1)
                nc.vector.tensor_tensor(t[0], y, y, ALU.mult).then_inc(newton_chain, 1)
                dve.wait_ge(newton_chain, 3 * n + 1)
                nc.vector.tensor_tensor(t[1], t[0], var_eps[:, :], ALU.mult).then_inc(newton_chain, 1)
                dve.wait_ge(newton_chain, 3 * n + 2)
                nc.vector.tensor_scalar(t[2], t[1], -0.5, 1.5, ALU.mult, ALU.add).then_inc(newton_chain, 1)
                dve.wait_ge(newton_chain, 3 * n + 3)
                nc.vector.tensor_tensor(rstd[:, :], y, t[2], ALU.mult).then_inc(rstd_ready, 1)

            def body(b):
                for k in range(STEPS):
                    q, c = divmod(k, SC)
                    nb, nq = (b, q + 1) if q < QUADS - 1 else (b + 1, 0)
                    if exists(nb) and (nq == 0 or exists(b)):
                        first = sum(FINDS_AT[:c])
                        for n in range(first, first + FINDS_AT[c]):
                            search(nb, nq, n)
                        if FINDS_AT[c] and first + FINDS_AT[c] == FINDS:
                            split_max(nb, nq)
                    for kind, index, n in side_units(b, k):
                        take(kind, index, n)
                    if c == 0:
                        pq = QUADS * b + q
                        if (q == 0 and exists(b - 1)) or (q > 0 and exists(b)):
                            dve.wait_ge(mixed_done, STEPS * b + k)
                            wait(dve, full["O"], pq - 1)
                            nc.vector.tensor_copy(mixed_sb[:, :], mixed[:, 0:T]).then_inc(mixed_taken, 1)
                    if exists(b + 1):
                        if k in STATS_AT:
                            if k == 1:
                                dve.wait_ge(audio_in, DMA * AUDIO_DMAS * (b + 2))
                                wait(dve, normed, SC * (b + 1))
                            for m in STATS_AT[k]:
                                statistics(b + 1, m)
                            for m in STATS_AT[k]:
                                aggregate(b + 1, m)
                        if k == NORM_STEP:
                            dve.wait_ge(moments, SC * (b + 2))
                            nc.vector.tensor_scalar(var_eps[:, :], mean_var[:, :, 1], EPS, None, ALU.add)\
                                .then_inc(eps_added, 1)
                        if k == NORM_STEP + 1:
                            refine(b + 1)

            run_batches(dve, body)

        @block.gpsimd
        def _(pool):
            nc.gpsimd.memset(ident[:, :], 0.0).then_inc(ident0, 1)
            pool.wait_ge(ident0, 1)
            nc.gpsimd.affine_select(out=ident[:, :], in_=ident[:, :], compare_op=ALU.not_equal, fill=1.0,
                                    base=0, pattern=[[-1, P]], channel_multiplier=1).then_inc(ident_ready, 1)
            pool.wait_ge(ident_ready, 1)
            nc.gpsimd.memset(k_rows[0:ROWS, :, S:SPAD], 0.0).then_inc(pool_ready, 1)
            pool.wait_ge(pool_ready, 1)
            two_ones = struct.unpack("<f", struct.pack("<I", 0x3F803F80))[0]
            for q in range(QUADS):
                if q > 0:
                    pool.wait_ge(ones_ready, q)
                rows = k_rows[MASK_ROW:ALL_ROWS, QUAD * q:QUAD * (q + 1), :].rearrange("p h s -> p (h s)")
                nc.gpsimd.memset(rows.bitcast(F32), two_ones).then_inc(ones_ready, 1)
            pool.wait_ge(ones_ready, QUADS)

            def mask_columns(n, index):
                chunks = [c for c in (2 * index, 2 * index + 1) if c < SC]
                if index == 0:
                    pool.wait_ge(mask_col, n + 1)
                wait(pool, mixed_done, STEPS * (n - 1) + SC * (QUADS - 1) + chunks[-1] + 1)
                own_instruction(pool)
                lo, hi = chunks[0], chunks[-1] + 1
                nc.gpsimd.tensor_copy(v_rows[:, lo:hi, :, HD],
                                      mask_c[:, lo:hi].unsqueeze(2).broadcast_to([P, hi - lo, HEADS]))\
                    .then_inc(v_mask, 1)

            def body(b):
                if exists(b):
                    mask_columns(b, PER["V"] - 1)
                if not exists(b + 1):
                    return
                n = b + 1
                pool.wait_ge(taken["QP"], n + 1)
                own_instruction(pool)
                nc.gpsimd.tensor_copy(q_parts[:, 1, :], q_rest[:, :]).then_inc(q_mid, 1)
                pool.wait_ge(q_mid, n + 1)
                nc.gpsimd.tensor_tensor(q_parts[:, 2, :], q_rest[:, :], q_parts[:, 1, :], ALU.subtract)\
                    .then_inc(q_split, 1)
                pool.wait_ge(eps_added, n + 1)
                nc.gpsimd.tensor_tensor(rstd0[:, :], var_eps[:, :], minus_half[:, :], ALU.pow)\
                    .then_inc(powered, 1)
                pool.wait_ge(rstd_ready, n + 1)
                own_instruction(pool)
                for c in range(SC):
                    nc.gpsimd.tensor_scalar(audio[:, c, :], audio[:, c, :], mean_var[:, c, 0:1],
                                            rstd[:, c:c + 1], ALU.subtract, ALU.mult).then_inc(normed, 1)
                wait(pool, taken["V"], PER["V"] * n)
                wait(pool, v_mask, PER["V"] * n)
                if as_int(b) == -1:
                    pool.wait_ge(taken["MT"], 1)
                own_instruction(pool)
                nc.gpsimd.tensor_copy(mask_c[:, 0:SC - 1], mask_t[:, bass.ds(n * (SC - 1), SC - 1)])
                nc.gpsimd.tensor_copy(mask_c[:, SC - 1:SC], mask_t[:, bass.ds(n + B * (SC - 1), 1)])\
                    .then_inc(mask_col, 1)
                for u in range(PER["K"]):
                    half, piece = divmod(u, PIECES)
                    lo, hi = CUTS[piece], CUTS[piece + 1]
                    rest = k_rest[:, u % RESID, 0:hi - lo]
                    pool.wait_ge(taken["K"], PER["K"] * n + u + 1)
                    own_instruction(pool)
                    nc.gpsimd.tensor_copy(k_parts[:, half, 1, lo:hi], rest).then_inc(k_mid, 1)
                    pool.wait_ge(k_mid, PER["K"] * n + u + 1)
                    nc.gpsimd.tensor_tensor(k_parts[:, half, 2, lo:hi], rest, k_parts[:, half, 1, lo:hi],
                                            ALU.subtract).then_inc(k_split, 1)
                for index in range(PER["V"] - 1):
                    mask_columns(n, index)

            run_batches(pool, body)


_INS = ["x", "ctx_2048", "mask_BxS2_bf1", "L0_xattn_Wq", "L0_xattn_Wk", "L0_xattn_Wv", "L0_xattn_Wo",
        "L0_xattn_ln_gamma", "L0_xattn_ln_beta", "L0_xattn_gate"]


def kernel(**inputs):
    import concourse.bacc as bacc
    from concourse.bass_utils import run_bass_kernel_spmd

    nc = bacc.Bacc("TRN2", target_bir_lowering=False, num_devices=1)
    arrays, args = {}, []
    for name in _INS:
        a = np.ascontiguousarray(inputs[name])
        arrays[f"in_{name}"] = a
        args.append(nc.dram_tensor(f"in_{name}", a.shape, mybir.dt.from_np(a.dtype), kind="ExternalInput").ap())
    out = nc.dram_tensor("out_dram", (B, T, D), F32, kind="ExternalOutput").ap()
    xattn_kernel(nc, *args, out)
    r = run_bass_kernel_spmd(nc, [arrays], core_ids=[0])
    return r.results[0]["out_dram"]
```

```python
import struct
from contextlib import ExitStack

import numpy as np

import concourse.bass as bass
from concourse import mybir

ALU = mybir.AluOpType
ACT = mybir.ActivationFunctionType
AX = mybir.AxisListType
F32 = mybir.dt.float32
BF16 = mybir.dt.bfloat16
U8 = mybir.dt.uint8

P = 128
B, T, S, D = 8, 256, 1601, 256
HEADS, HD = 16, 16
SCALE = HD ** -0.5
EPS = 1e-5
MASKED = -1e30

TC = T // P
DC = D // P
SC = -(-S // P)
SPAD = SC * P
SLAST = S - (SC - 1) * P
QUAD = 4
QUADS = HEADS // QUAD
STEPS = QUADS * SC
PARTS = 3
ROWS = 6 * HD
MASK_ROW = ROWS
MAX_ROWS = ROWS + 1
ALL_ROWS = ROWS + 1 + PARTS
K_PARTS = (0, 0, 0, 1, 1, 2)
Q_PARTS = (0, 1, 2, 0, 1, 0)
PIECES = 4
CUTS = [0, 401, 801, 1201, S]
FINDS = QUAD * TC * PIECES
PROBS = 4
RESID = 4
KHALF = 2

LEAD = 17
SEARCHES = sorted(
    ((SC * q - LEAD + n * SC // FINDS) % STEPS, q, n, (SC * q - LEAD + n * SC // FINDS < 0) * 1)
    for q in range(QUADS) for n in range(FINDS)
)
SEARCHES.sort(key=lambda f: (f[0], f[3], f[1], f[2]))

UNITS = sorted(
    [(0, "V", 6, 0), (1, "O", 3, -1), (3, "A", 0, -1), (5, "F", 0, -1)]
    + [(SC * (q + 1) + 1, "O", q, 0) for q in range(QUADS - 1)]
    + [(SC * q + 10 + u, "M", 2 * ((q + 1) % QUADS) + u, (q + 1) // QUADS) for q in range(QUADS) for u in range(2)]
    + [(4, "QT", 0, 1), (6, "QP", 0, 1)]
    + [(s, "XT", n, 1) for n, s in enumerate((13, 15, 16, 17, 18, 19, 20))]
    + [(s, "K", n, 1) for n, s in enumerate((21, 22, 25, 26, 28, 30, 32, 34))]
    + [(SC * (QUADS - 1) + 2 * n + 2, "V", n, 1) for n in range(6)],
    key=lambda u: u[0],
)
PER = {k: sum(u[1] == k for u in UNITS) for k in {u[1] for u in UNITS}}
NORMS = {"DVE": [c for c in range(SC) if c % 4 < 2], "Pool": [c for c in range(SC) if c % 4 >= 2]}
STATS_AT = {n: [2 * n + i for i in range(2) if 2 * n + i < SC] for n in range((SC + 1) // 2)}
EPS_STEP = len(STATS_AT) + 1
REFINE_STEP = EPS_STEP + 2


SCORE_BANKS, FOUND_BANKS, SIDE_BANKS = 3, 3, 1
HALVES = 2 * STEPS
PE_ORDER = "AfBfsfm"


def last_use(entries, at, banks, b):
    for back in range(0, 2):
        for n in range(at - 1 if back == 0 else len(entries) - 1, -1, -1):
            if n % banks == at % banks and 0 <= b - back + entries[n][3] < B:
                return n, -back
    return None


def xattn_kernel(nc, x, ctx, mask, wq, wk, wv, wo, gamma, beta, gate, out):
    with ExitStack() as stack:
        def sb(name, shape, dt=F32):
            return stack.enter_context(nc.sbuf_tensor(name, shape, dt))

        def ps(name, shape, dt=F32):
            return stack.enter_context(nc.psum_tensor(name, shape, dt))

        def sem(name):
            return stack.enter_context(nc.semaphore(name))

        k_scratch = nc.dram_tensor("k_scratch", (PARTS, HEADS * HD, S), BF16, kind="Internal").ap()
        q_scratch = nc.dram_tensor("q_scratch", (PARTS, HEADS * HD, T), BF16, kind="Internal").ap()
        bias_scratch = nc.dram_tensor("bias_scratch", (B, SPAD), BF16, kind="Internal").ap()

        scores = ps("scores", [P, SCORE_BANKS, 2 * T])
        found = ps("found", [P, FOUND_BANKS, 512])
        mixed = ps("mixed", [P, 512])
        sides = ps("sides", [P, SIDE_BANKS, 512])

        k_rows = sb("k_rows", [P, HEADS, SPAD], BF16)
        q_rows = sb("q_rows", [P, HEADS, T], BF16)
        v_rows = sb("v_rows", [P, SC, HEADS, HD + 1])
        probs = sb("probs", [P, PROBS, QUAD * T])
        audio = sb("audio", [P, SC, D])
        audio_t = sb("audio_t", [P, DC, S])
        k_parts = sb("k_parts", [P, KHALF, PARTS, S], BF16)
        k_rest = sb("k_rest", [P, RESID, 512])
        text = sb("text", [P, TC, D])
        text_t = sb("text_t", [P, DC, T])
        q_parts = sb("q_parts", [P, PARTS, KHALF * T], BF16)
        q_rest = sb("q_rest", [P, KHALF * T])
        w_in = sb("w_in", [P, 4, DC, D])
        w_t = sb("w_t", [P, 4, DC, D])
        ident = sb("ident", [P, P])
        ident_bf = sb("ident_bf", [P, P], BF16)
        gamma_c = sb("gamma_c", [P, DC])
        beta_c = sb("beta_c", [P, DC])
        gate_c = sb("gate_c", [P, 1])
        tanh_gate = sb("tanh_gate", [P, 1])
        mask_u8 = sb("mask_u8", [B, S], U8)
        bias_bf = sb("bias_bf", [B, SPAD], BF16)
        mask_tiles = sb("mask_tiles", [B * SC, P], U8)
        mask_f = sb("mask_f", [B * SC, P])
        mask_t = sb("mask_t", [P, B * SC])
        mask_c = sb("mask_c", [P, SC])
        bn = sb("bn", [P, SC, 6])
        mean_var = sb("mean_var", [P, SC, 2])
        var_eps = sb("var_eps", [P, SC])
        minus_half = sb("minus_half", [P, SC])
        rstd0 = sb("rstd0", [P, SC])
        newton = sb("newton", [P, 3, SC])
        rstd = sb("rstd", [P, SC])
        piece_max = sb("piece_max", [P, QUAD * TC, PIECES])
        neg_max = sb("neg_max", [P, QUAD * TC])
        neg_rest = sb("neg_rest", [P, QUAD * TC])
        neg_parts = sb("neg_parts", [P, QUAD * TC, 1 + PARTS], BF16)
        mixed_sb = sb("mixed_sb", [P, T])
        inv_sum = sb("inv_sum", [P, TC, QUAD])
        attn = sb("attn", [P, TC, D])
        attn_t = sb("attn_t", [P, DC * TC, P])
        residual = sb("residual", [P, TC, D])
        result = sb("result", [P, TC, D])

        full = {k: sem(f"full_{k}") for k in [*PER, "W", "MT"]}
        taken = {k: sem(f"taken_{k}") for k in [*PER, "W", "MT"]}
        scores_full = sem("scores_full")
        probs_ready = sem("probs_ready")
        mixed_done = sem("mixed_done")
        mixed_taken = sem("mixed_taken")
        found_full = sem("found_full")
        found_taken = sem("found_taken")
        max_chain = sem("max_chain")
        max_parts = sem("max_parts")
        inverted = sem("inverted")
        k_high = sem("k_high")
        q_high = sem("q_high")
        k_mid = sem("k_mid")
        q_mid = sem("q_mid")
        k_split = sem("k_split")
        q_split = sem("q_split")
        stats = sem("stats")
        moments = sem("moments")
        eps_added = sem("eps_added")
        powered = sem("powered")
        newton_chain = sem("newton_chain")
        rstd_ready = sem("rstd_ready")
        normed = {"Pool": sem("normed_pool"), "DVE": sem("normed_dve")}
        mask_col = sem("mask_col")
        v_mask = sem("v_mask")
        audio_in = sem("audio_in")
        text_in = sem("text_in")
        residual_in = sem("residual_in")
        stored = sem("stored")
        k_stored = [sem(f"k_stored{h}") for h in range(KHALF)]
        q_stored = sem("q_stored")
        quad_in = [sem(f"quad_in{q}") for q in range(QUADS)]
        w_loaded = sem("w_loaded")
        consts_in = sem("consts_in")
        mask_in = sem("mask_in")
        bias_stored = sem("bias_stored")
        ident0 = sem("ident0")
        ident_ready = sem("ident_ready")
        ident_bf_ready = sem("ident_bf_ready")
        tiles_zero = sem("tiles_zero")
        audio_pad = sem("audio_pad")
        bias_ready = sem("bias_ready")
        bias_pad = sem("bias_pad")
        mask_f_ready = sem("mask_f_ready")
        pool_ready = sem("pool_ready")
        ones_ready = sem("ones_ready")
        dve_ready = sem("dve_ready")
        gate_ready = sem("gate_ready")

        passed = sem("passed")

        DMA = 16
        QUAD_DMAS = 13
        AUDIO_DMAS = 4

        def wait(eng, semaphore, value):
            if isinstance(value, int) and value <= 0:
                return
            eng.wait_ge(semaphore, value)

        def own_instruction(eng):
            eng.sem_inc(passed, 1)

        def wait_apart(eng, semaphore, value):
            if isinstance(value, int) and value <= 0:
                return
            eng.wait_ge(semaphore, value)
            if not isinstance(value, int):
                own_instruction(eng)

        def exists(b):
            return not isinstance(b, int) or 0 <= b < B

        def as_int(b):
            return b if isinstance(b, int) else 1

        def run_batches(eng, body):
            body(-1)
            body(0)
            with eng.Fori(1, B - 1) as b:
                body(b)
            body(B - 1)
            body(B)

        def side_units(b, k):
            return [(u[1], u[2], b + u[3], at) for at, u in enumerate(UNITS)
                    if u[0] == k and 0 <= as_int(b) + u[3] < B]

        def side_bank(at):
            return sides[:, at % SIDE_BANKS, :]

        def searches(b, k):
            return [(b + d, q, n, at) for at, (s, q, n, d) in enumerate(SEARCHES)
                    if s == k and 0 <= as_int(b) + d < B]

        def normalise(engine, who, c):
            engine.tensor_scalar(audio[:, c, :], audio[:, c, :], mean_var[:, c, 0:1], rstd[:, c:c + 1],
                                 ALU.subtract, ALU.mult).then_inc(normed[who], 1)

        block = stack.enter_context(nc.Block())

        def load_audio(sp, b):
            wait_apart(sp, full["XT"], PER["XT"] * b)
            if isinstance(b, int) and b == 0:
                sp.wait_ge(audio_pad, 1)
            for c in range(0, SC - 1, 4):
                sp.dma_start(audio[:, c:c + 4, :],
                             ctx[b, c * P:(c + 4) * P, :].rearrange("(c p) d -> p c d", p=P))\
                  .then_inc(audio_in, DMA)
            sp.dma_start(audio[0:SLAST, SC - 1, :], ctx[b, (SC - 1) * P:S, :]).then_inc(audio_in, DMA)

        def load_text(sp, b):
            wait_apart(sp, full["QT"], b)
            sp.dma_start(text[:, :, :], x[b].rearrange("(c p) d -> p c d", p=P)).then_inc(text_in, DMA)

        @block.sync
        def _(sp):
            for n, w in enumerate((wk, wv, wq, wo)):
                sp.dma_start(w_in[:, n], w.rearrange("(c p) d -> p c d", p=P)).then_inc(w_loaded, DMA)
            load_audio(sp, 0)
            load_text(sp, 0)
            sp.dma_start(mask_u8[:, :], mask).then_inc(mask_in, DMA)
            sp.wait_ge(tiles_zero, 1)
            whole = (SC - 1) * P
            for b in range(B):
                sp.dma_start(mask_tiles[b * (SC - 1):(b + 1) * (SC - 1), :],
                             mask[b, 0:whole].rearrange("(c p) -> c p", p=P)).then_inc(mask_in, DMA)
            sp.dma_start(mask_tiles[B * (SC - 1):B * SC, 0:SLAST], mask[:, whole:S]).then_inc(mask_in, DMA)
            sp.wait_ge(bias_ready, 1)
            sp.dma_start(bias_scratch, bias_bf[:, :]).then_inc(bias_stored, DMA)
            sp.wait_ge(bias_stored, DMA)

            def load_quad(b, q):
                wait_apart(sp, scores_full, HALVES * (b - 1) + 2 * SC * (q + 1))
                if as_int(b) == 0:
                    sp.wait_ge(ones_ready, q + 1)
                slots = slice(QUAD * q, QUAD * (q + 1))
                lines = slice(QUAD * HD * q, QUAD * HD * (q + 1))
                for g in range(6):
                    sp.dma_start(k_rows[HD * g:HD * (g + 1), slots, 0:S],
                                 k_scratch[K_PARTS[g], lines, :].rearrange("(h d) s -> d h s", d=HD))\
                      .then_inc(quad_in[q], DMA)
                for g in range(6):
                    sp.dma_start(q_rows[HD * g:HD * (g + 1), slots, :],
                                 q_scratch[Q_PARTS[g], lines, :].rearrange("(h d) t -> d h t", d=HD))\
                      .then_inc(quad_in[q], DMA)
                sp.dma_start(k_rows[MASK_ROW:MASK_ROW + 1, slots, :],
                             bias_scratch[bass.ds(b, 1), :].unsqueeze(1).broadcast_to([1, QUAD, SPAD]))\
                  .then_inc(quad_in[q], DMA)

            def body(b):
                if exists(b + 1) and as_int(b) >= 0:
                    load_audio(sp, b + 1)
                    load_text(sp, b + 1)
                if exists(b):
                    load_quad(b, QUADS - 1)
                if exists(b - 1):
                    wait_apart(sp, taken["F"], b)
                    sp.dma_start(out[b - 1].rearrange("(c p) d -> p c d", p=P), result[:, :, :])\
                      .then_inc(stored, DMA)
                if exists(b):
                    wait_apart(sp, taken["F"], b)
                    sp.dma_start(residual[:, :, :], x[b].rearrange("(c p) d -> p c d", p=P))\
                      .then_inc(residual_in, DMA)
                if exists(b + 1):
                    n = b + 1
                    wait_apart(sp, q_split, n + 1)
                    for q in range(QUADS):
                        wait_apart(sp, quad_in[q], DMA * QUAD_DMAS * n)
                    for half in range(KHALF):
                        sp.dma_start(q_scratch[:, P * half:P * (half + 1), :].rearrange("a p t -> p a t"),
                                     q_parts[:, :, T * half:T * (half + 1)]).then_inc(q_stored, DMA)
                    for half in range(KHALF):
                        wait_apart(sp, k_split, PER["K"] * n + PIECES * (half + 1))
                        sp.dma_start(k_scratch[:, P * half:P * (half + 1), :].rearrange("a p s -> p a s"),
                                     k_parts[:, half]).then_inc(k_stored[half], DMA)
                        if half == 0:
                            wait_apart(sp, q_stored, DMA * KHALF * (n + 1))
                        wait_apart(sp, k_stored[half], DMA * (n + 1))
                        for q in (2 * half, 2 * half + 1):
                            if q < QUADS - 1:
                                load_quad(n, q)

            run_batches(sp, body)
            sp.wait_ge(stored, DMA * B)

        @block.tensor
        def _(pe):
            pe.wait_ge(ident_ready, 1)
            pe.wait_ge(w_loaded, 4 * DMA)
            side = side_bank(0)
            for n in range(4):
                wait(pe, taken["W"], n)
                for i in range(DC):
                    for o in range(DC):
                        mm = nc.tensor.transpose(side[:, D * i + P * o:D * i + P * (o + 1)],
                                                 w_in[:, n, o, P * i:P * (i + 1)], ident[:, :])
                mm.then_inc(full["W"], 1)
            pe.wait_ge(taken["W"], 4)
            pe.wait_ge(mask_f_ready, 1)
            nc.tensor.transpose(side[:, 0:B * SC], mask_f[:, :], ident[0:B * SC, 0:B * SC])\
                .then_inc(full["MT"], 1)
            pe.wait_ge(ident_bf_ready, 1)
            pe.wait_ge(dve_ready, 1)
            pe.wait_ge(pool_ready, 1)

            def free_side(b, at):
                last = last_use(UNITS, at, SIDE_BANKS, as_int(b))
                if last is None:
                    pe.wait_ge(taken["MT"], 1)
                else:
                    _, kind, index, d = UNITS[last[0]]
                    pe.wait_ge(taken[kind], PER[kind] * (b + last[1] + d) + index + 1)

            def unit(kind, index, n, at):
                side = side_bank(at)
                if kind == "V":
                    chunks = [c for c in (2 * index, 2 * index + 1) if c < SC]
                    for c in chunks:
                        rows = P if c < SC - 1 else SLAST
                        for i in range(DC):
                            mm = nc.tensor.matmul(side[0:rows, D * (c % 2):D * (c % 2 + 1)],
                                                  audio_t[:, i, P * c:P * c + rows], w_t[:, 1, i, :],
                                                  start=(i == 0), stop=(i == DC - 1))
                elif kind == "K":
                    half, piece = divmod(index, PIECES)
                    if index == 0:
                        pe.wait_ge(taken["XT"], PER["XT"] * (n + 1))
                    lo, hi = CUTS[piece], CUTS[piece + 1]
                    for i in range(DC):
                        mm = nc.tensor.matmul(side[:, 0:hi - lo], w_t[:, 0, i, P * half:P * (half + 1)],
                                              audio_t[:, i, lo:hi], start=(i == 0), stop=(i == DC - 1))
                elif kind == "XT":
                    if index < PER["XT"] - 1:
                        group, i = divmod(index, DC)
                        for who, chunks in NORMS.items():
                            done = sum(c < 4 * group + 4 for c in chunks)
                            pe.wait_ge(normed[who], len(chunks) * n + done)
                        for c in range(4):
                            mm = nc.tensor.transpose(side[:, P * c:P * (c + 1)],
                                                     audio[:, 4 * group + c, P * i:P * (i + 1)], ident[:, :])
                    else:
                        for who, chunks in NORMS.items():
                            pe.wait_ge(normed[who], len(chunks) * (n + 1))
                        for i in range(DC):
                            mm = nc.tensor.transpose(side[:, P * i:P * i + SLAST],
                                                     audio[0:SLAST, SC - 1, P * i:P * (i + 1)],
                                                     ident[0:SLAST, 0:SLAST])
                elif kind == "QT":
                    pe.wait_ge(text_in, DMA * (n + 1))
                    for i in range(DC):
                        for c in range(TC):
                            mm = nc.tensor.transpose(side[:, T * i + P * c:T * i + P * (c + 1)],
                                                     text[:, c, P * i:P * (i + 1)], ident[:, :])
                elif kind == "QP":
                    for half in range(KHALF):
                        for i in range(DC):
                            mm = nc.tensor.matmul(side[:, T * half:T * (half + 1)],
                                                  w_t[:, 2, i, P * half:P * (half + 1)], text_t[:, i, :],
                                                  start=(i == 0), stop=(i == DC - 1))
                elif kind == "M":
                    q, u = divmod(index, 2)
                    if u == 0:
                        pe.wait_ge(max_parts, QUADS * n + q + 1)
                    for m in range(2 * TC):
                        mm = nc.tensor.matmul(side[MASK_ROW:ALL_ROWS, P * m:P * (m + 1)],
                                              neg_parts[:, 2 * TC * u + m, :], ident_bf[:, :],
                                              start=True, stop=True)
                elif kind == "O":
                    pe.wait_ge(mixed_taken, QUADS * n + index + 1)
                    for c in range(TC):
                        mm = nc.tensor.transpose(side[:, P * c:P * (c + 1)],
                                                 mixed_sb[:, P * c:P * (c + 1)], ident[:, :])
                elif kind == "A":
                    pe.wait_ge(taken["O"], QUADS * (n + 1))
                    for i in range(DC):
                        for c in range(TC):
                            m = TC * i + c
                            mm = nc.tensor.transpose(side[:, P * m:P * (m + 1)],
                                                     attn[:, c, P * i:P * (i + 1)], ident[:, :])
                else:
                    for c in range(TC):
                        for i in range(DC):
                            mm = nc.tensor.matmul(side[:, D * c:D * (c + 1)], attn_t[:, TC * i + c, :],
                                                  w_t[:, 3, i, :], start=(i == 0), stop=(i == DC - 1))
                mm.then_inc(full[kind], 1)

            def score(b, k, half):
                q, c = divmod(k, SC)
                at = 2 * k + half
                last = [n for n in range(at - HALVES, at) if n % HALVES % SCORE_BANKS == at % SCORE_BANKS][-1]
                wait(pe, probs_ready, HALVES * b + last + 1)
                if c == 0 and half == 0:
                    pe.wait_ge(taken["M"], 2 * (QUADS * b + q + 1))
                for j in range(2):
                    h = QUAD * q + 2 * half + j
                    mm = nc.tensor.matmul(scores[:, at % SCORE_BANKS, T * j:T * (j + 1)],
                                          k_rows[0:ALL_ROWS, h, P * c:P * (c + 1)],
                                          q_rows[0:ALL_ROWS, h, :], start=True, stop=True)
                mm.then_inc(scores_full, 1)

            def find(b, body_b, q, n, at):
                if n == 0:
                    pe.wait_ge(quad_in[q], DMA * QUAD_DMAS * (b + 1))
                last = last_use(SEARCHES, at, FOUND_BANKS, as_int(body_b))
                if last is not None:
                    _, lq, ln, d = SEARCHES[last[0]]
                    pe.wait_ge(found_taken, FINDS * (QUADS * (body_b + last[1] + d) + lq) + ln + 1)
                j, c, piece = n // (TC * PIECES), n // PIECES % TC, n % PIECES
                h = QUAD * q + j
                lo, hi = CUTS[piece], CUTS[piece + 1]
                nc.tensor.matmul(found[:, at % FOUND_BANKS, 0:hi - lo], q_rows[0:MAX_ROWS, h, P * c:P * (c + 1)],
                                 k_rows[0:MAX_ROWS, h, lo:hi], start=True, stop=True)\
                    .then_inc(found_full, 1)

            def mix(b, k):
                q, c = divmod(k, SC)
                pe.wait_ge(probs_ready, HALVES * b + 2 * k + 2)
                if c == 0:
                    wait(pe, mixed_taken, QUADS * b + q)
                if q == 0 and c % 2 == 0:
                    pe.wait_ge(taken["V"], PER["V"] * b + c // 2 + 1)
                    pe.wait_ge(v_mask, PER["V"] * b + c // 2 + 1)
                for j in range(QUAD):
                    mm = nc.tensor.matmul(mixed[32 * j:32 * j + HD + 1, 0:T], v_rows[:, c, QUAD * q + j, :],
                                          probs[:, k % PROBS, T * j:T * (j + 1)],
                                          start=(c == 0), stop=(c == SC - 1))
                mm.then_inc(mixed_done, 1)

            def body(b):
                for k in range(STEPS):
                    finds = iter(searches(b, k))
                    for what in PE_ORDER + "f" * FINDS:
                        if what in "AB" and exists(b):
                            score(b, k, "AB".index(what))
                        if what == "f":
                            search = next(finds, None)
                            if search is not None:
                                batch, q, n, at = search
                                find(batch, b, q, n, at)
                        if what == "s":
                            for kind, index, n, at in side_units(b, k):
                                free_side(b, at)
                                unit(kind, index, n, at)
                        if what == "m" and k > 0 and exists(b):
                            mix(b, k - 1)
                        if what == "m" and k == 0 and exists(b - 1):
                            mix(b - 1, STEPS - 1)

            run_batches(pe, body)

        @block.scalar
        def _(act):
            act.dma_start(gamma_c[:, :], gamma.rearrange("(c p) -> p c", p=P),
                          allow_slow_non_contiguous=True).then_inc(consts_in, DMA)
            act.dma_start(beta_c[:, :], beta.rearrange("(c p) -> p c", p=P),
                          allow_slow_non_contiguous=True).then_inc(consts_in, DMA)
            act.dma_start(gate_c[:, :], gate.partition_broadcast(P)).then_inc(consts_in, DMA)
            act.wait_ge(consts_in, 3 * DMA)
            nc.scalar.activation(tanh_gate[:, :], gate_c[:, :], ACT.Tanh).then_inc(gate_ready, 1)
            act.wait_ge(pool_ready, 1)
            act.wait_ge(dve_ready, 1)

            def take(kind, index, n, at):
                side = side_bank(at)
                if kind == "XT":
                    act.wait_ge(full["XT"], PER["XT"] * n + index + 1)
                    if index < PER["XT"] - 1:
                        group, i = divmod(index, DC)
                        spans = [(i, 4 * P * group, 4 * P, 0)]
                    else:
                        spans = [(i, P * (SC - 1), SLAST, P * i) for i in range(DC)]
                    for i, to, width, frm in spans:
                        last = nc.scalar.activation(audio_t[:, i, to:to + width], side[:, frm:frm + width],
                                                    ACT.Identity, bias=beta_c[:, i:i + 1],
                                                    scale=gamma_c[:, i:i + 1])
                    last.then_inc(taken["XT"], 1)
                elif kind == "QT":
                    act.wait_ge(full["QT"], n + 1)
                    nc.scalar.activation(text_t[:, :, :].rearrange("p i t -> p (i t)"), side[:, 0:DC * T],
                                         ACT.Copy).then_inc(taken["QT"], 1)
                elif kind == "QP":
                    act.wait_ge(full["QP"], n + 1)
                    wait(act, q_stored, DMA * KHALF * n)
                    nc.scalar.activation(q_parts[:, 0, :], side[:, :], ACT.Copy, scale=SCALE)\
                        .then_inc(q_high, 1)
                elif kind == "K":
                    half, piece = divmod(index, PIECES)
                    act.wait_ge(full["K"], PER["K"] * n + index + 1)
                    if piece == 0:
                        wait(act, k_stored[half], DMA * n)
                    lo, hi = CUTS[piece], CUTS[piece + 1]
                    nc.scalar.activation(k_parts[:, half, 0, lo:hi], side[:, 0:hi - lo], ACT.Copy)\
                        .then_inc(k_high, 1)
                elif kind == "V":
                    act.wait_ge(full["V"], PER["V"] * n + index + 1)
                    if index == 0:
                        act.wait_ge(mask_col, n + 1)
                    chunks = [c for c in (2 * index, 2 * index + 1) if c < SC]
                    wait(act, mixed_done, STEPS * (n - 1) + SC * (QUADS - 1) + chunks[-1] + 1)
                    for c in chunks:
                        rows = P if c < SC - 1 else SLAST
                        last = nc.scalar.activation(
                            v_rows[0:rows, c, :, 0:HD],
                            side[0:rows, D * (c % 2):D * (c % 2 + 1)].rearrange("p (h d) -> p h d", d=HD),
                            ACT.Copy, scale=mask_c[0:rows, c:c + 1])
                    last.then_inc(taken["V"], 1)
                elif kind == "M":
                    q, u = divmod(index, 2)
                    act.wait_ge(full["M"], PER["M"] * n + index + 1)
                    h = QUAD * q + 2 * u
                    nc.scalar.activation(q_rows[MASK_ROW:ALL_ROWS, h:h + 2, :].rearrange("p h t -> p (h t)"),
                                         side[MASK_ROW:ALL_ROWS, :], ACT.Copy).then_inc(taken["M"], 1)
                elif kind == "A":
                    act.wait_ge(full["A"], n + 1)
                    nc.scalar.activation(attn_t[:, :, :].rearrange("p m t -> p (m t)"), side[:, :], ACT.Copy)\
                        .then_inc(taken["A"], 1)

            def body(b):
                for k in range(STEPS):
                    if exists(b):
                        wait(act, mixed_done, STEPS * b + k - PROBS + 1)
                        for half in range(2):
                            at = 2 * k + half
                            act.wait_ge(scores_full, HALVES * b + at + 1)
                            nc.scalar.activation(probs[:, k % PROBS, 2 * T * half:2 * T * (half + 1)],
                                                 scores[:, at % SCORE_BANKS, :], ACT.Exp)\
                                .then_inc(probs_ready, 1)
                    for unit in side_units(b, k):
                        take(*unit)

            run_batches(act, body)

        @block.vector
        def _(dve):
            nc.vector.memset(mask_tiles[:, :], 0).then_inc(tiles_zero, 1)
            nc.vector.memset(bias_bf[:, :], MASKED).then_inc(bias_pad, 1)
            nc.vector.memset(audio[64:P, SC - 1, :], 0.0).then_inc(audio_pad, 1)
            nc.vector.memset(mean_var[:, :, :], 1.0)
            nc.vector.memset(minus_half[:, :], -0.5)
            nc.vector.memset(q_rows[MASK_ROW:ALL_ROWS, :, :], 1.0)
            nc.vector.memset(neg_parts[:, :, :], 1.0)
            nc.vector.memset(v_rows[64:P, SC - 1], 0.0)
            nc.vector.memset(mixed[:, :], 0.0).then_inc(dve_ready, 1)
            dve.wait_ge(ident_ready, 1)
            nc.vector.tensor_copy(ident_bf[:, :], ident[:, :]).then_inc(ident_bf_ready, 1)
            dve.wait_ge(mask_in, DMA * (B + 2))
            dve.wait_ge(bias_pad, 1)
            nc.vector.tensor_scalar(bias_bf[:, 0:S], mask_u8[:, :], -1.0, -MASKED, ALU.add, ALU.mult)\
                .then_inc(bias_ready, 1)
            nc.vector.tensor_copy(mask_f[:, :], mask_tiles[:, :]).then_inc(mask_f_ready, 1)
            side = side_bank(0)
            for n in range(4):
                dve.wait_ge(full["W"], n + 1)
                nc.vector.tensor_copy(w_t[:, n].rearrange("p i o -> p (i o)"), side[:, :]).then_inc(taken["W"], 1)
            dve.wait_ge(full["MT"], 1)
            nc.vector.tensor_copy(mask_t[:, :], side[:, 0:B * SC]).then_inc(taken["MT"], 1)
            dve.wait_ge(gate_ready, 1)

            def search(b, q, n, at):
                quad = QUADS * b + q
                piece = n % PIECES
                width = CUTS[piece + 1] - CUTS[piece]
                dve.wait_ge(found_full, FINDS * quad + n + 1)
                nc.vector.tensor_reduce(piece_max[:, n // PIECES, piece:piece + 1], found[:, at % FOUND_BANKS, 0:width],
                                        AX.X, ALU.max).then_inc(found_taken, 1)

            def split_max(b, q):
                quad = QUADS * b + q
                dve.wait_ge(found_taken, FINDS * (quad + 1))
                nc.vector.tensor_reduce(neg_max[:, :], piece_max[:, :, :], AX.X, ALU.max, negate=True)\
                    .then_inc(max_chain, 1)
                wait(dve, full["M"], 2 * quad)
                dve.wait_ge(max_chain, 4 * quad + 1)
                nc.vector.tensor_copy(neg_parts[:, :, 1], neg_max[:, :]).then_inc(max_chain, 1)
                dve.wait_ge(max_chain, 4 * quad + 2)
                nc.vector.tensor_tensor(neg_rest[:, :], neg_max[:, :], neg_parts[:, :, 1], ALU.subtract)\
                    .then_inc(max_chain, 1)
                dve.wait_ge(max_chain, 4 * quad + 3)
                nc.vector.tensor_copy(neg_parts[:, :, 2], neg_rest[:, :]).then_inc(max_chain, 1)
                dve.wait_ge(max_chain, 4 * quad + 4)
                nc.vector.tensor_tensor(neg_parts[:, :, 3], neg_rest[:, :], neg_parts[:, :, 2], ALU.subtract)\
                    .then_inc(max_parts, 1)

            def take(kind, index, n, at):
                side = side_bank(at)
                if kind == "K":
                    dve.wait_ge(k_high, PER["K"] * n + index + 1)
                    wait(dve, k_split, PER["K"] * n + index + 1 - RESID)
                    half, piece = divmod(index, PIECES)
                    lo, hi = CUTS[piece], CUTS[piece + 1]
                    nc.vector.tensor_tensor(k_rest[:, index % RESID, 0:hi - lo], side[:, 0:hi - lo],
                                            k_parts[:, half, 0, lo:hi], ALU.subtract).then_inc(taken["K"], 1)
                elif kind == "QP":
                    dve.wait_ge(q_high, n + 1)
                    nc.vector.scalar_tensor_tensor(q_rest[:, :], side[:, :], SCALE, q_parts[:, 0, :],
                                                   ALU.mult, ALU.subtract).then_inc(taken["QP"], 1)
                elif kind == "O":
                    quad = QUADS * n + index
                    dve.wait_ge(full["O"], quad + 1)
                    sums = side[:, 0:TC * P].rearrange("p (c j e) -> p c j e", c=TC, j=QUAD)
                    nc.vector.reciprocal(inv_sum[:, :, :], sums[:, :, :, HD]).then_inc(inverted, 1)
                    dve.wait_ge(inverted, quad + 1)
                    width = QUAD * HD
                    nc.vector.tensor_tensor(
                        attn[:, :, width * index:width * (index + 1)].rearrange("p c (j d) -> p c j d", j=QUAD),
                        sums[:, :, :, 0:HD],
                        inv_sum[:, :, :].unsqueeze(3).broadcast_to([P, TC, QUAD, HD]),
                        ALU.mult).then_inc(taken["O"], 1)
                elif kind == "F":
                    dve.wait_ge(full["F"], n + 1)
                    dve.wait_ge(residual_in, DMA * (n + 1))
                    wait(dve, stored, DMA * n)
                    nc.vector.scalar_tensor_tensor(
                        result[:, :, :].rearrange("p c d -> p (c d)"), side[:, :], tanh_gate[:, 0:1],
                        residual[:, :, :].rearrange("p c d -> p (c d)"), ALU.mult, ALU.add)\
                        .then_inc(taken["F"], 1)

            def statistics(n, c):
                rows = P if c < SC - 1 else SLAST
                nc.vector.bn_stats(bn[0:rows, c, :], audio[0:rows, c, :]).then_inc(stats, 1)

            def aggregate(n, c):
                rows = P if c < SC - 1 else SLAST
                dve.wait_ge(stats, SC * n + c + 1)
                own_instruction(dve)
                nc.vector.bn_aggr(mean_var[0:rows, c, :], bn[0:rows, c, :]).then_inc(moments, 1)

            def add_eps(n):
                dve.wait_ge(moments, SC * (n + 1))
                nc.vector.tensor_scalar(var_eps[:, :], mean_var[:, :, 1], EPS, None, ALU.add)\
                    .then_inc(eps_added, 1)

            def normalise_own(n, c):
                if c == NORMS["DVE"][0]:
                    dve.wait_ge(rstd_ready, n + 1)
                normalise(nc.vector, "DVE", c)

            def refine(n):
                y, t = rstd0[:, :], [newton[:, i, :] for i in range(3)]
                dve.wait_ge(powered, n + 1)
                nc.vector.tensor_tensor(t[0], y, y, ALU.mult).then_inc(newton_chain, 1)
                dve.wait_ge(newton_chain, 3 * n + 1)
                nc.vector.tensor_tensor(t[1], t[0], var_eps[:, :], ALU.mult).then_inc(newton_chain, 1)
                dve.wait_ge(newton_chain, 3 * n + 2)
                nc.vector.tensor_scalar(t[2], t[1], -0.5, 1.5, ALU.mult, ALU.add).then_inc(newton_chain, 1)
                dve.wait_ge(newton_chain, 3 * n + 3)
                nc.vector.tensor_tensor(rstd[:, :], y, t[2], ALU.mult).then_inc(rstd_ready, 1)

            def normalisation(b, k):
                n = b + 1
                if not exists(n):
                    return []
                pieces = []
                if k == 0:
                    dve.wait_ge(audio_in, DMA * AUDIO_DMAS * (n + 1))
                    wait(dve, normed["Pool"], len(NORMS["Pool"]) * n)
                pieces += [lambda c=c: statistics(n, c) for c in STATS_AT.get(k, ())]
                pieces += [lambda c=c: aggregate(n, c) for c in STATS_AT.get(k - 1, ())]
                if k == EPS_STEP:
                    pieces.append(lambda: add_eps(n))
                if k == REFINE_STEP:
                    pieces.append(lambda: refine(n))
                first = 2 * (k - REFINE_STEP - 1)
                if first >= 0:
                    pieces += [lambda c=c: normalise_own(n, c) for c in NORMS["DVE"][first:first + 2]]
                return pieces

            def body(b):
                for k in range(STEPS):
                    pieces = normalisation(b, k)
                    for nb, nq, n, at in searches(b, k):
                        search(nb, nq, n, at)
                        if n == FINDS - 1:
                            split_max(nb, nq)
                        if pieces:
                            pieces.pop(0)()
                    for unit in side_units(b, k):
                        take(*unit)
                    if k % SC == 0:
                        quad = QUADS * b + k // SC - 1
                        if exists(b - 1) if k == 0 else exists(b):
                            dve.wait_ge(mixed_done, STEPS * b + k)
                            wait(dve, full["O"], quad)
                            nc.vector.tensor_copy(mixed_sb[:, :], mixed[:, 0:T]).then_inc(mixed_taken, 1)
                    for piece in pieces:
                        piece()

            run_batches(dve, body)

        @block.gpsimd
        def _(pool):
            nc.gpsimd.memset(ident[:, :], 0.0).then_inc(ident0, 1)
            pool.wait_ge(ident0, 1)
            nc.gpsimd.affine_select(out=ident[:, :], in_=ident[:, :], compare_op=ALU.not_equal, fill=1.0,
                                    base=0, pattern=[[-1, P]], channel_multiplier=1).then_inc(ident_ready, 1)
            pool.wait_ge(ident_ready, 1)
            nc.gpsimd.memset(k_rows[0:ROWS, :, S:SPAD], 0.0).then_inc(pool_ready, 1)
            pool.wait_ge(pool_ready, 1)
            two_ones = struct.unpack("<f", struct.pack("<I", 0x3F803F80))[0]
            for q in range(QUADS):
                if q > 0:
                    pool.wait_ge(ones_ready, q)
                rows = k_rows[MASK_ROW:ALL_ROWS, QUAD * q:QUAD * (q + 1), :].rearrange("p h s -> p (h s)")
                nc.gpsimd.memset(rows.bitcast(F32), two_ones).then_inc(ones_ready, 1)
            pool.wait_ge(ones_ready, QUADS)

            def mask_columns(n, index):
                chunks = [c for c in (2 * index, 2 * index + 1) if c < SC]
                if index == 0:
                    pool.wait_ge(mask_col, n + 1)
                wait(pool, mixed_done, STEPS * (n - 1) + SC * (QUADS - 1) + chunks[-1] + 1)
                own_instruction(pool)
                lo, hi = chunks[0], chunks[-1] + 1
                nc.gpsimd.tensor_copy(v_rows[:, lo:hi, :, HD],
                                      mask_c[:, lo:hi].unsqueeze(2).broadcast_to([P, hi - lo, HEADS]))\
                    .then_inc(v_mask, 1)

            def body(b):
                if exists(b):
                    mask_columns(b, PER["V"] - 1)
                if not exists(b + 1):
                    return
                n = b + 1
                pool.wait_ge(taken["QP"], n + 1)
                own_instruction(pool)
                nc.gpsimd.tensor_copy(q_parts[:, 1, :], q_rest[:, :]).then_inc(q_mid, 1)
                pool.wait_ge(q_mid, n + 1)
                nc.gpsimd.tensor_tensor(q_parts[:, 2, :], q_rest[:, :], q_parts[:, 1, :], ALU.subtract)\
                    .then_inc(q_split, 1)
                pool.wait_ge(eps_added, n + 1)
                nc.gpsimd.tensor_tensor(rstd0[:, :], var_eps[:, :], minus_half[:, :], ALU.pow)\
                    .then_inc(powered, 1)
                pool.wait_ge(rstd_ready, n + 1)
                own_instruction(pool)
                for c in NORMS["Pool"]:
                    normalise(nc.gpsimd, "Pool", c)
                wait(pool, taken["V"], PER["V"] * n)
                wait(pool, v_mask, PER["V"] * n)
                if as_int(b) == -1:
                    pool.wait_ge(taken["MT"], 1)
                own_instruction(pool)
                nc.gpsimd.tensor_copy(mask_c[:, 0:SC - 1], mask_t[:, bass.ds(n * (SC - 1), SC - 1)])
                nc.gpsimd.tensor_copy(mask_c[:, SC - 1:SC], mask_t[:, bass.ds(n + B * (SC - 1), 1)])\
                    .then_inc(mask_col, 1)
                for u in range(PER["K"]):
                    half, piece = divmod(u, PIECES)
                    lo, hi = CUTS[piece], CUTS[piece + 1]
                    rest = k_rest[:, u % RESID, 0:hi - lo]
                    pool.wait_ge(taken["K"], PER["K"] * n + u + 1)
                    own_instruction(pool)
                    nc.gpsimd.tensor_copy(k_parts[:, half, 1, lo:hi], rest).then_inc(k_mid, 1)
                    pool.wait_ge(k_mid, PER["K"] * n + u + 1)
                    nc.gpsimd.tensor_tensor(k_parts[:, half, 2, lo:hi], rest, k_parts[:, half, 1, lo:hi],
                                            ALU.subtract).then_inc(k_split, 1)
                for index in range(PER["V"] - 1):
                    mask_columns(n, index)

            run_batches(pool, body)


_INS = ["x", "ctx_2048", "mask_BxS2_bf1", "L0_xattn_Wq", "L0_xattn_Wk", "L0_xattn_Wv", "L0_xattn_Wo",
        "L0_xattn_ln_gamma", "L0_xattn_ln_beta", "L0_xattn_gate"]


def kernel(**inputs):
    import concourse.bacc as bacc
    from concourse.bass_utils import run_bass_kernel_spmd

    nc = bacc.Bacc("TRN2", target_bir_lowering=False, num_devices=1)
    arrays, args = {}, []
    for name in _INS:
        a = np.ascontiguousarray(inputs[name])
        arrays[f"in_{name}"] = a
        args.append(nc.dram_tensor(f"in_{name}", a.shape, mybir.dt.from_np(a.dtype), kind="ExternalInput").ap())
    out = nc.dram_tensor("out_dram", (B, T, D), F32, kind="ExternalOutput").ap()
    xattn_kernel(nc, *args, out)
    r = run_bass_kernel_spmd(nc, [arrays], core_ids=[0])
    return r.results[0]["out_dram"]
```

```python
import struct
from contextlib import ExitStack

import numpy as np

import concourse.bass as bass
from concourse import mybir

ALU = mybir.AluOpType
ACT = mybir.ActivationFunctionType
AX = mybir.AxisListType
F32 = mybir.dt.float32
BF16 = mybir.dt.bfloat16
U8 = mybir.dt.uint8
F32R = mybir.dt.float32r

P = 128
B, T, S, D = 8, 256, 1601, 256
HEADS, HD = 16, 16
SCALE = HD ** -0.5
EPS = 1e-5
MASKED = -1e30

TC = T // P
DC = D // P
SC = -(-S // P)
SPAD = SC * P
SLAST = S - (SC - 1) * P
QUAD = 4
QUADS = HEADS // QUAD
STEPS = QUADS * SC
PARTS = 3
ROWS = 6 * HD
MASK_ROW = ROWS
MAX_ROWS = ROWS + 1
ALL_ROWS = ROWS + 1 + PARTS
K_PARTS = (0, 1, 2, 0, 1, 0)
Q_PARTS = (0, 1, 0, 1, 0, 2)
PIECES = 4
S_EVEN = S + S % 2
CUTS = [min(2 * -(-S_EVEN * p // (2 * PIECES)), S) for p in range(PIECES + 1)]
FINDS = QUAD * TC * PIECES
LINKS = 5
PROBS = 4
WHOLE = 3
RESID = 4
DMA = 16
AUDIO_DMAS = -(-SC // 4)
KHALF = 2

LEAD = 18
SEARCHES = sorted(
    ((SC * q - LEAD + n * SC // FINDS) % STEPS, q, n, (SC * q - LEAD + n * SC // FINDS < 0) * 1)
    for q in range(QUADS) for n in range(FINDS)
)
SEARCHES.sort(key=lambda f: (f[0], f[3], f[1], f[2]))

LAST_SEARCH = max(s for s, q, n, d in SEARCHES if q == QUADS - 1 and d == 0)
UNITS = sorted(
    [(0, "V", 6, 0), (1, "O", QUADS - 1, -1), (3, "A", 0, -1), (5, "F", 0, -1)]
    + [(SC * (q + 1) + 1, "O", q, 0) for q in range(QUADS - 1)]
    + [(SC * q + 10 + u, "M", 2 * ((q + 1) % QUADS) + u, (q + 1) // QUADS) for q in range(QUADS) for u in range(2)]
    + [(4, "QT", 0, 1), (8, "QP", 0, 1)]
    + [(s, "XT", n, 1) for n, s in enumerate((13, 15, 16, 17, 19, 20, 22))]
    + [(s, "K", n, 1) for n, s in enumerate((18, 21, 25, 25, 29, 30, 31, 33))]
    + [(s, "V", n, 1) for n, s in enumerate((42, 45, 46, 48, 49, 51))],
    key=lambda u: u[0],
)
FIRST_UNITS = [at for at, u in enumerate(UNITS) if u[3] == 1]
PER = {k: sum(u[1] == k for u in UNITS) for k in {u[1] for u in UNITS}}
NORMS = {"DVE": [c for c in range(SC) if c % 4 < 3], "Pool": [c for c in range(SC) if c % 4 == 3]}
STATS_AT = {n: [2 * n + i for i in range(2) if 2 * n + i < SC] for n in range((SC + 1) // 2)}
EPS_STEP = len(STATS_AT)
AUDIO_SPLIT_STEP = 16
REFINE_STEP = EPS_STEP + 2


SCORE_BANKS, FOUND_BANKS, SIDE_BANKS = 2, 3, 2
HALVES = 2 * STEPS
PE_ORDER = "fAfBfsm"


def runs(parts):
    starts = [g for g in range(len(parts)) if g == 0 or parts[g] != parts[g - 1] + 1]
    return [(g, parts[g], end - g) for g, end in zip(starts, starts[1:] + [len(parts)])]


QUAD_DMAS = len(runs(K_PARTS)) + len(runs(Q_PARTS)) + 1


def first_slot(at):
    return FIRST_UNITS.index(at) % (SIDE_BANKS + SCORE_BANKS)


def last_first_unit(slot, before=len(UNITS)):
    return [at for at in FIRST_UNITS if first_slot(at) == slot and at < before][-1:]


def last_use(entries, at, banks, b):
    for back in range(0, 2):
        for n in range(at - 1 if back == 0 else len(entries) - 1, -1, -1):
            if n % banks == at % banks and 0 <= b - back + entries[n][3] < B:
                return n, -back
    return None


def xattn_kernel(nc, x, ctx, mask, wq, wk, wv, wo, gamma, beta, gate, out):
    with ExitStack() as stack:
        def sb(name, shape, dt=F32):
            return stack.enter_context(nc.sbuf_tensor(name, shape, dt))

        def ps(name, shape, dt=F32):
            return stack.enter_context(nc.psum_tensor(name, shape, dt))

        def sem(name):
            return stack.enter_context(nc.semaphore(name))

        k_scratch = nc.dram_tensor("k_scratch", (QUADS, PARTS, HD * QUAD, S), BF16, kind="Internal").ap()
        q_scratch = nc.dram_tensor("q_scratch", (QUADS, PARTS, HD * QUAD, T), BF16, kind="Internal").ap()
        bias_scratch = nc.dram_tensor("bias_scratch", (B, SPAD), BF16, kind="Internal").ap()

        scores = ps("scores", [P, SCORE_BANKS, 2 * T])
        found = ps("found", [P, FOUND_BANKS, 512])
        mixed = ps("mixed", [P, 512])
        sides = ps("sides", [P, SIDE_BANKS, 512])

        k_rows = sb("k_rows", [P, HEADS, SPAD], BF16)
        q_rows = sb("q_rows", [P, HEADS, T], BF16)
        v_rows = sb("v_rows", [P, SC, HEADS, HD + 1])
        probs = sb("probs", [P, PROBS, QUAD * T])
        audio = sb("audio", [P, SC, D])
        audio_hi = sb("audio_hi", [P, DC, S_EVEN], F32R)
        audio_lo = sb("audio_lo", [P, DC, S_EVEN], F32R)
        audio_t = sb("audio_t", [P, WHOLE, 4 * P])
        k_parts = sb("k_parts", [P, KHALF, PARTS, S], BF16)
        k_rest = sb("k_rest", [P, RESID, 512])
        text = sb("text", [P, TC, D])
        text_t = sb("text_t", [P, DC, T])
        q_parts = sb("q_parts", [P, PARTS, KHALF * T], BF16)
        q_rest = sb("q_rest", [P, KHALF * T])
        w_in = probs[:, 0:4, 0:DC * D].rearrange("p n (c d) -> p n c d", c=DC)
        w_t = sb("w_t", [P, 2, DC, D])
        w_hi = sb("w_hi", [P, 2, DC, D], F32R)
        w_lo = sb("w_lo", [P, 2, DC, D], F32R)
        ident = sb("ident", [P, P])
        ident_bf = sb("ident_bf", [P, P], BF16)
        gamma_c = sb("gamma_c", [P, DC])
        beta_c = sb("beta_c", [P, DC])
        gate_c = sb("gate_c", [P, 1])
        tanh_gate = sb("tanh_gate", [P, 1])
        mask_u8 = sb("mask_u8", [B, S], U8)
        bias_bf = sb("bias_bf", [B, SPAD], BF16)
        mask_f = sb("mask_f", [B, SPAD])
        mask_t = sb("mask_t", [P, SC, B])
        mask_c = sb("mask_c", [P, SC])
        bn = sb("bn", [P, SC, 6])
        mean_var = sb("mean_var", [P, SC, 2])
        var_eps = sb("var_eps", [P, SC])
        minus_half = sb("minus_half", [P, SC])
        rstd0 = sb("rstd0", [P, SC])
        newton = sb("newton", [P, 3, SC])
        rstd = sb("rstd", [P, SC])
        piece_max = sb("piece_max", [P, 2, QUAD * TC, PIECES])
        neg_max = sb("neg_max", [P, QUAD * TC])
        neg_rest = sb("neg_rest", [P, QUAD * TC])
        neg_parts = sb("neg_parts", [P, QUAD * TC, 1 + PARTS], BF16)
        mixed_sb = sb("mixed_sb", [P, T])
        inv_sum = sb("inv_sum", [P, TC, QUAD])
        attn = sb("attn", [P, TC, D])
        attn_t = sb("attn_t", [P, DC * TC, P])
        residual = sb("residual", [P, TC, D])
        result = sb("result", [P, TC, D])

        full = {k: sem(f"full_{k}") for k in [*PER, "W", "MT"]}
        taken = {k: sem(f"taken_{k}") for k in [*PER, "W", "MT"]}
        scores_full = sem("scores_full")
        probs_ready = sem("probs_ready")
        mixed_done = sem("mixed_done")
        mixed_taken = sem("mixed_taken")
        found_full = sem("found_full")
        found_taken = sem("found_taken")
        max_chain = sem("max_chain")
        max_parts = sem("max_parts")
        inverted = sem("inverted")
        even_pad = sem("even_pad")
        w_low = sem("w_low")
        audio_low = sem("audio_low")
        k_high = sem("k_high")
        q_high = sem("q_high")
        k_mid = sem("k_mid")
        q_mid = sem("q_mid")
        k_split = sem("k_split")
        q_split = sem("q_split")
        stats = sem("stats")
        moments = sem("moments")
        eps_added = sem("eps_added")
        powered = sem("powered")
        newton_chain = sem("newton_chain")
        rstd_ready = sem("rstd_ready")
        normed = {"Pool": sem("normed_pool"), "DVE": sem("normed_dve")}
        mask_col = sem("mask_col")
        v_mask = sem("v_mask")
        audio_in = [sem(f"audio_in{g}") for g in range(AUDIO_DMAS)]
        text_in = sem("text_in")
        residual_in = sem("residual_in")
        stored = sem("stored")
        k_stored = [sem(f"k_stored{q}") for q in range(QUADS)]
        q_stored = sem("q_stored")
        quad_in = [sem(f"quad_in{q}") for q in range(QUADS)]
        w_loaded = [sem(f"w_loaded{n}") for n in range(4)]
        consts_in = sem("consts_in")
        mask_in = sem("mask_in")
        bias_stored = sem("bias_stored")
        ident0 = sem("ident0")
        ident_ready = sem("ident_ready")
        ident_bf_ready = sem("ident_bf_ready")
        audio_pad = sem("audio_pad")
        bias_ready = sem("bias_ready")
        mask_pad = sem("mask_pad")
        mask_f_ready = sem("mask_f_ready")
        pool_ready = sem("pool_ready")
        ones_ready = sem("ones_ready")
        dve_ready = sem("dve_ready")
        gate_ready = sem("gate_ready")

        passed = sem("passed")

        def wait(eng, semaphore, value):
            if isinstance(value, int) and value <= 0:
                return
            eng.wait_ge(semaphore, value)

        def own_instruction(eng):
            eng.sem_inc(passed, 1)

        def stores_of_k(q, batches):
            return DMA * (batches + (PIECES - 1) * (q == 0))

        def wait_apart(eng, semaphore, value):
            if isinstance(value, int) and value <= 0:
                return
            eng.wait_ge(semaphore, value)
            if not isinstance(value, int):
                own_instruction(eng)

        def exists(b):
            return not isinstance(b, int) or 0 <= b < B

        def as_int(b):
            return b if isinstance(b, int) else 1

        def run_batches(eng, body):
            body(-1)
            body(0)
            with eng.Fori(1, B - 1) as b:
                body(b)
            body(B - 1)
            body(B)

        def side_units(b, k):
            return [(u[1], u[2], b + u[3], at) for at, u in enumerate(UNITS)
                    if u[0] == k and 0 <= as_int(b) + u[3] < B]

        def is_first(n, at):
            return isinstance(n, int) and n == 0 and UNITS[at][3] == 1

        def side_bank(at, n):
            if not is_first(n, at):
                return sides[:, at % SIDE_BANKS, :]
            slot = first_slot(at)
            return sides[:, slot, :] if slot < SIDE_BANKS else scores[:, slot - SIDE_BANKS, :]

        def searches(b, k):
            return [(b + d, q, n, at) for at, (s, q, n, d) in enumerate(SEARCHES)
                    if s == k and 0 <= as_int(b) + d < B]

        def split_q(eng, engine, n):
            engine.tensor_copy(q_parts[:, 1, :], q_rest[:, :]).then_inc(q_mid, 1)
            eng.wait_ge(q_mid, n + 1)
            engine.tensor_tensor(q_parts[:, 2, :], q_rest[:, :], q_parts[:, 1, :], ALU.subtract)\
                .then_inc(q_split, 1)

        def split_k(eng, engine, n, index):
            half, piece = divmod(index, PIECES)
            lo, hi = CUTS[piece], CUTS[piece + 1]
            rest = k_rest[:, index % RESID, 0:hi - lo]
            engine.tensor_copy(k_parts[:, half, 1, lo:hi], rest).then_inc(k_mid, 1)
            eng.wait_ge(k_mid, PER["K"] * n + index + 1)
            engine.tensor_tensor(k_parts[:, half, 2, lo:hi], rest, k_parts[:, half, 1, lo:hi],
                                 ALU.subtract).then_inc(k_split, 1)

        def split_audio(engine, index):
            group, i = divmod(index, DC)
            whole = audio_t[:, index % WHOLE, :]
            if index < PER["XT"] - 1:
                where = (slice(0, P), i, slice(4 * P * group, 4 * P * (group + 1)))
            else:
                where = (slice(0, P), slice(0, DC), slice(P * (SC - 1), S))
                whole = whole[:, 0:DC * SLAST].rearrange("p (i s) -> p i s", i=DC)
            engine.tensor_tensor(audio_lo[where], whole, audio_hi[where].bitcast(F32),
                                 ALU.subtract).then_inc(audio_low, 1)

        def project(out, stationary, moving):
            products = [(i, a, b) for i in range(DC) for a, b in ((0, 0), (0, 1), (1, 0))]
            for at, (i, a, b) in enumerate(products):
                mm = nc.tensor.matmul(out, stationary(a, i), moving(b, i),
                                      start=(at == 0), stop=(at == len(products) - 1))
            return mm

        def weight_bank(n):
            return (found[:, 1, :], found[:, 2, :], scores[:, 0, :], scores[:, 1, :])[n]

        def by_head(n, i):
            return weight_bank(n)[:, D * i:D * (i + 1)].rearrange("p (q h d) -> p q h d", q=QUADS, h=QUAD)

        def by_dimension(tile):
            return tile.rearrange("p (q d h) -> p q h d", q=QUADS, h=QUAD)

        def normalise(engine, who, c):
            engine.tensor_scalar(audio[:, c, :], audio[:, c, :], mean_var[:, c, 0:1], rstd[:, c:c + 1],
                                 ALU.subtract, ALU.mult).then_inc(normed[who], 1)

        block = stack.enter_context(nc.Block())

        def load_audio(sp, b, groups=range(AUDIO_DMAS)):
            wait_apart(sp, full["XT"], PER["XT"] * b)
            for g in groups:
                if g < AUDIO_DMAS - 1:
                    sp.dma_start(audio[:, 4 * g:4 * g + 4, :],
                                 ctx[b, 4 * P * g:4 * P * (g + 1), :].rearrange("(c p) d -> p c d", p=P))\
                      .then_inc(audio_in[g], DMA)
                else:
                    if isinstance(b, int) and b == 0:
                        sp.wait_ge(audio_pad, 1)
                    sp.dma_start(audio[0:SLAST, SC - 1, :], ctx[b, (SC - 1) * P:S, :])\
                      .then_inc(audio_in[g], DMA)

        def load_text(sp, b):
            wait_apart(sp, full["QT"], b)
            sp.dma_start(text[:, :, :], x[b].rearrange("(c p) d -> p c d", p=P)).then_inc(text_in, DMA)

        @block.sync
        def _(sp):
            def load_weight(n):
                sp.dma_start(w_in[:, n], (wk, wv, wq, wo)[n].rearrange("(c p) d -> p c d", p=P))\
                  .then_inc(w_loaded[n], DMA)

            load_audio(sp, 0, [0])
            load_weight(2)
            load_text(sp, 0)
            load_audio(sp, 0, range(1, AUDIO_DMAS))
            sp.dma_start(mask_u8[:, :], mask).then_inc(mask_in, DMA)
            for n in (0, 1, 3):
                load_weight(n)
            sp.wait_ge(bias_ready, 1)
            sp.dma_start(bias_scratch, bias_bf[:, :]).then_inc(bias_stored, DMA)

            def load_q(b, q):
                wait_apart(sp, scores_full, HALVES * (b - 1) + 2 * SC * (q + 1))
                for g, part, n in runs(Q_PARTS):
                    sp.dma_start(q_rows[HD * g:HD * (g + n), QUAD * q:QUAD * (q + 1), :],
                                 q_scratch[q, part:part + n].rearrange("a (d h) t -> (a d) h t", h=QUAD))\
                      .then_inc(quad_in[q], DMA)

            def load_k(b, q):
                slots = slice(QUAD * q, QUAD * (q + 1))
                for g, part, n in runs(K_PARTS):
                    sp.dma_start(k_rows[HD * g:HD * (g + n), slots, 0:S],
                                 k_scratch[q, part:part + n].rearrange("a (d h) s -> (a d) h s", h=QUAD))\
                      .then_inc(quad_in[q], DMA)
                if isinstance(b, int) and b == 0:
                    sp.wait_ge(bias_stored, DMA)
                    sp.wait_ge(ones_ready, q + 1)
                sp.dma_start(k_rows[MASK_ROW:MASK_ROW + 1, slots, :],
                             bias_scratch[bass.ds(b, 1), :].unsqueeze(1).broadcast_to([1, QUAD, SPAD]))\
                  .then_inc(quad_in[q], DMA)

            def body(b):
                if exists(b + 1) and as_int(b) >= 0:
                    load_audio(sp, b + 1)
                    load_text(sp, b + 1)
                if exists(b):
                    if as_int(b) > 0:
                        load_q(b, QUADS - 1)
                    load_k(b, QUADS - 1)
                if exists(b - 1):
                    wait_apart(sp, taken["F"], b)
                    sp.dma_start(out[b - 1].rearrange("(c p) d -> p c d", p=P), result[:, :, :])\
                      .then_inc(stored, DMA)
                if exists(b):
                    wait_apart(sp, taken["F"], b)
                    sp.dma_start(residual[:, :, :], x[b].rearrange("(c p) d -> p c d", p=P))\
                      .then_inc(residual_in, DMA)
                if exists(b + 1):
                    n = b + 1
                    wait_apart(sp, q_split, n + 1)
                    for q in range(QUADS):
                        wait_apart(sp, quad_in[q], DMA * QUAD_DMAS * n)
                    for q in range(QUADS):
                        half, rows = q // 2, slice(P // 2 * (q % 2), P // 2 * (q % 2 + 1))
                        sp.dma_start(q_scratch[q].rearrange("a r t -> r a t"),
                                     q_parts[rows, :, T * half:T * (half + 1)]).then_inc(q_stored, DMA)
                    wait_apart(sp, q_stored, DMA * QUADS * (n + 1))
                    early = range(QUADS if as_int(b) == -1 else 1)
                    for q in early:
                        load_q(n, q)
                    def store_k(q, piece):
                        span = slice(0, S) if piece is None else slice(CUTS[piece], CUTS[piece + 1])
                        rows = slice(P // 2 * (q % 2), P // 2 * (q % 2 + 1))
                        sp.dma_start(k_scratch[q, :, :, span].rearrange("a r s -> r a s"),
                                     k_parts[rows, q // 2, :, span]).then_inc(k_stored[q], DMA)

                    for half in range(KHALF):
                        ahead = as_int(b) == -1 and half == 0
                        for piece in range(PIECES) if ahead else ():
                            sp.wait_ge(k_split, piece + 1)
                            store_k(0, piece)
                        wait_apart(sp, k_split, PER["K"] * n + PIECES * (half + 1))
                        for q in (2 * half, 2 * half + 1):
                            if not ahead:
                                store_k(q, None)
                        for q in (2 * half, 2 * half + 1):
                            if ahead and q == 1:
                                store_k(q, None)
                            wait_apart(sp, k_stored[q], stores_of_k(q, n + 1))
                            if q < QUADS - 1:
                                if q not in early:
                                    load_q(n, q)
                                load_k(n, q)

            run_batches(sp, body)
            sp.wait_ge(stored, DMA * B)

        @block.tensor
        def _(pe):
            pe.wait_ge(ident_ready, 1)

            def transpose_weight(n):
                pe.wait_ge(w_loaded[n], DMA)
                for i in range(DC):
                    for o in range(DC):
                        mm = nc.tensor.transpose(weight_bank(n)[:, D * i + P * o:D * i + P * (o + 1)],
                                                 w_in[:, n, o, P * i:P * (i + 1)], ident[:, :])
                mm.then_inc(full["W"], 1)

            transpose_weight(2)

            def later_setup():
                for n in (0, 1, 3):
                    transpose_weight(n)
                pe.wait_ge(mask_f_ready, 1)
                for c in range(SC):
                    mm = nc.tensor.transpose(found[:, 0, B * c:B * (c + 1)], mask_f[:, P * c:P * (c + 1)],
                                             ident[0:B, 0:B])
                mm.then_inc(full["MT"], 1)
                pe.wait_ge(ident_bf_ready, 1)
                pe.wait_ge(dve_ready, 1)
                pe.wait_ge(pool_ready, 2)

            def free_first(at):
                _, kind, index, _ = UNITS[at]
                pe.wait_ge(taken[kind], index + 1)

            def free_side(b, at):
                if as_int(b) == -1:
                    slot = first_slot(at)
                    for last in last_first_unit(slot, at):
                        free_first(last)
                    if slot == SIDE_BANKS + 1:
                        pe.wait_ge(taken["W"], 4)
                    return
                last = last_use(UNITS, at, SIDE_BANKS, as_int(b))
                if as_int(b) == 0 and (last is None or last[1] < 0):
                    for first in last_first_unit(at % SIDE_BANKS):
                        free_first(first)
                elif last is not None:
                    _, kind, index, d = UNITS[last[0]]
                    pe.wait_ge(taken[kind], PER[kind] * (b + last[1] + d) + index + 1)

            def unit(kind, index, n, at):
                side = side_bank(at, n)
                if kind == "V":
                    chunks = [c for c in (2 * index, 2 * index + 1) if c < SC]
                    for c in chunks:
                        rows = P if c < SC - 1 else SLAST
                        mm = project(side[0:rows, D * (c % 2):D * (c % 2 + 1)],
                                     lambda part, i: (audio_hi, audio_lo)[part][:, i, P * c:P * c + rows],
                                     lambda part, i: (w_hi, w_lo)[part][:, 1, i, :])
                elif kind == "K":
                    half, piece = divmod(index, PIECES)
                    lo, hi = CUTS[piece], CUTS[piece + 1] + CUTS[piece + 1] % 2
                    if half == 0:
                        pe.wait_ge(audio_low, PER["XT"] * n + min(DC * -(-hi // (4 * P)), PER["XT"]))
                    if index == 0 and as_int(n) == 0:
                        pe.wait_ge(w_low, DC + 1)
                        pe.wait_ge(even_pad, 2)
                    mm = project(side[:, 0:hi - lo],
                                 lambda part, i: (w_hi, w_lo)[part][:, 0, i, P * half:P * (half + 1)],
                                 lambda part, i: (audio_hi, audio_lo)[part][:, i, lo:hi])
                elif kind == "XT":
                    if index < PER["XT"] - 1:
                        group, i = divmod(index, DC)
                        for who, chunks in NORMS.items():
                            done = sum(c < 4 * group + 4 for c in chunks)
                            pe.wait_ge(normed[who], len(chunks) * n + done)
                        for c in range(4):
                            mm = nc.tensor.transpose(side[:, P * c:P * (c + 1)],
                                                     audio[:, 4 * group + c, P * i:P * (i + 1)], ident[:, :])
                    else:
                        for who, chunks in NORMS.items():
                            pe.wait_ge(normed[who], len(chunks) * (n + 1))
                        for i in range(DC):
                            mm = nc.tensor.transpose(side[:, P * i:P * i + SLAST],
                                                     audio[0:SLAST, SC - 1, P * i:P * (i + 1)],
                                                     ident[0:SLAST, 0:SLAST])
                elif kind == "QT":
                    pe.wait_ge(text_in, DMA * (n + 1))
                    for i in range(DC):
                        for c in range(TC):
                            mm = nc.tensor.transpose(side[:, T * i + P * c:T * i + P * (c + 1)],
                                                     text[:, c, P * i:P * (i + 1)], ident[:, :])
                elif kind == "QP":
                    pe.wait_ge(taken["QT"], n + 1)
                    if as_int(n) == 0:
                        pe.wait_ge(taken["W"], 1)
                    for half in range(KHALF):
                        for i in range(DC):
                            mm = nc.tensor.matmul(side[:, T * half:T * (half + 1)],
                                                  w_t[:, 0, i, P * half:P * (half + 1)], text_t[:, i, :],
                                                  start=(i == 0), stop=(i == DC - 1))
                elif kind == "M":
                    q, u = divmod(index, 2)
                    if u == 0:
                        pe.wait_ge(max_parts, QUADS * n + q + 1)
                    for m in range(2 * TC):
                        mm = nc.tensor.matmul(side[MASK_ROW:ALL_ROWS, P * m:P * (m + 1)],
                                              neg_parts[:, 2 * TC * u + m, :], ident_bf[:, :],
                                              start=True, stop=True)
                elif kind == "O":
                    pe.wait_ge(mixed_taken, QUADS * n + index + 1)
                    for c in range(TC):
                        mm = nc.tensor.transpose(side[:, P * c:P * (c + 1)],
                                                 mixed_sb[:, P * c:P * (c + 1)], ident[:, :])
                elif kind == "A":
                    pe.wait_ge(taken["O"], QUADS * (n + 1))
                    for i in range(DC):
                        for c in range(TC):
                            m = TC * i + c
                            mm = nc.tensor.transpose(side[:, P * m:P * (m + 1)],
                                                     attn[:, c, P * i:P * (i + 1)], ident[:, :])
                else:
                    pe.wait_ge(taken["A"], n + 1)
                    for c in range(TC):
                        for i in range(DC):
                            mm = nc.tensor.matmul(side[:, D * c:D * (c + 1)], attn_t[:, TC * i + c, :],
                                                  w_t[:, 1, i, :], start=(i == 0), stop=(i == DC - 1))
                mm.then_inc(full[kind], 1)

            def score(b, k, half):
                q, c = divmod(k, SC)
                at = 2 * k + half
                last = [n for n in range(at - HALVES, at) if n % HALVES % SCORE_BANKS == at % SCORE_BANKS][-1]
                wait(pe, probs_ready, HALVES * b + last + 1)
                if as_int(b) == 0 and at < SCORE_BANKS:
                    for first in last_first_unit(SIDE_BANKS + at):
                        free_first(first)
                if c == 0 and half == 0:
                    pe.wait_ge(taken["M"], 2 * (QUADS * b + q + 1))
                for j in range(2):
                    h = QUAD * q + 2 * half + j
                    mm = nc.tensor.matmul(scores[:, at % SCORE_BANKS, T * j:T * (j + 1)],
                                          k_rows[0:ALL_ROWS, h, P * c:P * (c + 1)],
                                          q_rows[0:ALL_ROWS, h, :], start=True, stop=True)
                mm.then_inc(scores_full, 1)

            def find(b, body_b, q, n, at):
                if as_int(body_b) == -1 and n == 0:
                    pe.wait_ge(taken["MT"], 1)
                if n == 0:
                    pe.wait_ge(quad_in[q], DMA * QUAD_DMAS * (b + 1))
                last = last_use(SEARCHES, at, FOUND_BANKS, as_int(body_b))
                if last is not None:
                    _, lq, ln, d = SEARCHES[last[0]]
                    pe.wait_ge(found_taken, FINDS * (QUADS * (body_b + last[1] + d) + lq) + ln + 1)
                j, c, piece = n // (TC * PIECES), n // PIECES % TC, n % PIECES
                h = QUAD * q + j
                lo, hi = CUTS[piece], CUTS[piece + 1]
                nc.tensor.matmul(found[:, at % FOUND_BANKS, 0:hi - lo], q_rows[0:MAX_ROWS, h, P * c:P * (c + 1)],
                                 k_rows[0:MAX_ROWS, h, lo:hi], start=True, stop=True)\
                    .then_inc(found_full, 1)

            def mix(b, k):
                q, c = divmod(k, SC)
                pe.wait_ge(probs_ready, HALVES * b + 2 * k + 2)
                if c == 0:
                    wait(pe, mixed_taken, QUADS * b + q)
                if q == 0 and c % 2 == 0:
                    pe.wait_ge(taken["V"], PER["V"] * b + c // 2 + 1)
                    pe.wait_ge(v_mask, PER["V"] * b + c // 2 + 1)
                for j in range(QUAD):
                    mm = nc.tensor.matmul(mixed[32 * j:32 * j + HD + 1, 0:T], v_rows[:, c, QUAD * q + j, :],
                                          probs[:, k % PROBS, T * j:T * (j + 1)],
                                          start=(c == 0), stop=(c == SC - 1))
                mm.then_inc(mixed_done, 1)

            def body(b):
                for k in range(STEPS):
                    finds = iter(searches(b, k))
                    for what in PE_ORDER + "f" * FINDS:
                        if what in "AB" and exists(b):
                            score(b, k, "AB".index(what))
                        if what == "f":
                            search = next(finds, None)
                            if search is not None:
                                batch, q, n, at = search
                                find(batch, b, q, n, at)
                        if what == "s":
                            for kind, index, n, at in side_units(b, k):
                                free_side(b, at)
                                unit(kind, index, n, at)
                                if as_int(b) == -1 and kind == "QP":
                                    later_setup()
                        if what == "m" and k > 0 and exists(b):
                            mix(b, k - 1)
                        if what == "m" and k == 0 and exists(b - 1):
                            mix(b - 1, STEPS - 1)

            run_batches(pe, body)

        @block.scalar
        def _(act):
            act.dma_start(gamma_c[:, :], gamma.rearrange("(c p) -> p c", p=P),
                          allow_slow_non_contiguous=True).then_inc(consts_in, DMA)
            act.dma_start(beta_c[:, :], beta.rearrange("(c p) -> p c", p=P),
                          allow_slow_non_contiguous=True).then_inc(consts_in, DMA)
            act.dma_start(gate_c[:, :], gate.partition_broadcast(P)).then_inc(consts_in, DMA)
            act.wait_ge(consts_in, 3 * DMA)
            nc.scalar.activation(tanh_gate[:, :], gate_c[:, :], ACT.Tanh).then_inc(gate_ready, 1)

            def take_weight(n, count):
                act.wait_ge(full["W"], count)
                to = w_hi[:, n] if n < 2 else w_t[:, n - 2]
                if n in (1, 3):
                    last = nc.scalar.activation(to.rearrange("p i o -> p (i o)"), weight_bank(n), ACT.Copy)
                else:
                    for i in range(DC):
                        last = nc.scalar.activation(by_dimension(to[:, i]), by_head(n, i), ACT.Copy)
                last.then_inc(taken["W"], 1)

            take_weight(2, 1)

            def later_setup():
                for count, n in enumerate((0, 1, 3)):
                    take_weight(n, count + 2)
                act.wait_ge(mask_in, DMA)
                act.wait_ge(mask_pad, 1)
                nc.scalar.activation(mask_f[:, 0:S], mask_u8[:, :], ACT.Copy).then_inc(mask_f_ready, 1)
                act.wait_ge(mask_f_ready, 1)
                nc.scalar.activation(bias_bf[:, :], mask_f[:, :], ACT.Copy, bias=MASKED, scale=-MASKED)\
                    .then_inc(bias_ready, 1)
                act.wait_ge(full["MT"], 1)
                nc.scalar.activation(mask_t[:, :, :].rearrange("p c b -> p (c b)"), found[:, 0, 0:SC * B],
                                     ACT.Copy).then_inc(taken["MT"], 1)
                act.wait_ge(pool_ready, 2)
                act.wait_ge(dve_ready, 1)

            def take(kind, index, n, at):
                side = side_bank(at, n)
                if kind == "XT":
                    act.wait_ge(full["XT"], PER["XT"] * n + index + 1)
                    wait(act, audio_low, PER["XT"] * n + max(index + 1 - WHOLE, 0))
                    last_unit = index == PER["XT"] - 1
                    if not last_unit:
                        group, i = divmod(index, DC)
                        spans = [(i, 4 * P * group, 4 * P, 0)]
                    else:
                        spans = [(i, P * (SC - 1), SLAST, P * i) for i in range(DC)]
                    for i, to, width, frm in spans:
                        for tile in (audio_t[:, index % WHOLE, SLAST * i * last_unit:SLAST * i * last_unit + width], audio_hi[:, i, to:to + width]):
                            last = nc.scalar.activation(tile, side[:, frm:frm + width], ACT.Identity,
                                                        bias=beta_c[:, i:i + 1], scale=gamma_c[:, i:i + 1])
                    last.then_inc(taken["XT"], 1)
                elif kind == "QT":
                    act.wait_ge(full["QT"], n + 1)
                    nc.scalar.activation(text_t[:, :, :].rearrange("p i t -> p (i t)"), side[:, 0:DC * T],
                                         ACT.Copy).then_inc(taken["QT"], 1)
                elif kind == "QP":
                    act.wait_ge(full["QP"], n + 1)
                    wait(act, q_stored, DMA * QUADS * n)
                    nc.scalar.activation(q_parts[:, 0, :], side[:, :], ACT.Copy, scale=SCALE)\
                        .then_inc(q_high, 1)
                elif kind == "K":
                    half, piece = divmod(index, PIECES)
                    act.wait_ge(full["K"], PER["K"] * n + index + 1)
                    if piece == 0:
                        for q in (2 * half, 2 * half + 1):
                            if as_int(n) > 0:
                                act.wait_ge(k_stored[q], stores_of_k(q, n))
                    lo, hi = CUTS[piece], CUTS[piece + 1]
                    nc.scalar.activation(k_parts[:, half, 0, lo:hi], side[:, 0:hi - lo], ACT.Copy)\
                        .then_inc(k_high, 1)
                elif kind == "V":
                    act.wait_ge(full["V"], PER["V"] * n + index + 1)
                    if index == 0:
                        act.wait_ge(mask_col, n + 1)
                    chunks = [c for c in (2 * index, 2 * index + 1) if c < SC]
                    wait(act, mixed_done, STEPS * (n - 1) + SC * (QUADS - 1) + chunks[-1] + 1)
                    for c in chunks:
                        rows = P if c < SC - 1 else SLAST
                        last = nc.scalar.activation(
                            v_rows[0:rows, c, :, 0:HD],
                            side[0:rows, D * (c % 2):D * (c % 2 + 1)].rearrange("p (h d) -> p h d", d=HD),
                            ACT.Copy, scale=mask_c[0:rows, c:c + 1])
                    last.then_inc(taken["V"], 1)
                elif kind == "M":
                    q, u = divmod(index, 2)
                    act.wait_ge(full["M"], PER["M"] * n + index + 1)
                    h = QUAD * q + 2 * u
                    nc.scalar.activation(q_rows[MASK_ROW:ALL_ROWS, h:h + 2, :].rearrange("p h t -> p (h t)"),
                                         side[MASK_ROW:ALL_ROWS, :], ACT.Copy).then_inc(taken["M"], 1)
                elif kind == "A":
                    act.wait_ge(full["A"], n + 1)
                    nc.scalar.activation(attn_t[:, :, :].rearrange("p m t -> p (m t)"), side[:, :], ACT.Copy)\
                        .then_inc(taken["A"], 1)

            def body(b):
                for k in range(STEPS):
                    if exists(b):
                        wait(act, mixed_done, STEPS * b + k - PROBS + 1)
                        for half in range(2):
                            at = 2 * k + half
                            act.wait_ge(scores_full, HALVES * b + at + 1)
                            nc.scalar.activation(probs[:, k % PROBS, 2 * T * half:2 * T * (half + 1)],
                                                 scores[:, at % SCORE_BANKS, :], ACT.Exp)\
                                .then_inc(probs_ready, 1)
                    for unit in side_units(b, k):
                        take(*unit)
                        if as_int(b) == -1 and unit[0] == "QP":
                            later_setup()

            run_batches(act, body)

        @block.vector
        def _(dve):
            nc.vector.memset(mask_f[:, S:SPAD], 0.0).then_inc(mask_pad, 1)
            nc.vector.memset(audio[64:P, SC - 1, :], 0.0).then_inc(audio_pad, 1)
            nc.vector.memset(audio_hi[:, :, S:S_EVEN].bitcast(F32), 0.0).then_inc(even_pad, 1)
            nc.vector.memset(audio_lo[:, :, S:S_EVEN].bitcast(F32), 0.0).then_inc(even_pad, 1)
            nc.vector.memset(mean_var[:, :, :], 1.0)
            nc.vector.memset(minus_half[:, :], -0.5)
            nc.vector.memset(neg_parts[:, :, :], 1.0)
            nc.vector.memset(v_rows[64:P, SC - 1], 0.0)
            nc.vector.memset(mixed[:, :], 0.0).then_inc(dve_ready, 1)
            dve.wait_ge(dve_ready, 1)
            dve.wait_ge(ident_ready, 1)
            nc.vector.tensor_copy(ident_bf[:, :], ident[:, :]).then_inc(ident_bf_ready, 1)

            def search(b, q, n, at):
                quad = QUADS * b + q
                piece = n % PIECES
                width = CUTS[piece + 1] - CUTS[piece]
                dve.wait_ge(found_full, FINDS * quad + n + 1)
                nc.vector.tensor_reduce(piece_max[:, q % 2, n // PIECES, piece:piece + 1], found[:, at % FOUND_BANKS, 0:width],
                                        AX.X, ALU.max).then_inc(found_taken, 1)

            def split_max(b, q, link):
                quad = QUADS * b + q
                if link == 0:
                    dve.wait_ge(found_taken, FINDS * (quad + 1))
                    nc.vector.tensor_reduce(neg_max[:, :], piece_max[:, q % 2], AX.X, ALU.max, negate=True)\
                        .then_inc(max_chain, 1)
                    return
                if link == 1:
                    wait(dve, full["M"], 2 * quad)
                dve.wait_ge(max_chain, (LINKS - 1) * quad + link)
                if link == 1:
                    nc.vector.tensor_copy(neg_parts[:, :, 1], neg_max[:, :]).then_inc(max_chain, 1)
                elif link == 2:
                    nc.vector.tensor_tensor(neg_rest[:, :], neg_max[:, :], neg_parts[:, :, 1], ALU.subtract)\
                        .then_inc(max_chain, 1)
                elif link == 3:
                    nc.vector.tensor_copy(neg_parts[:, :, 2], neg_rest[:, :]).then_inc(max_chain, 1)
                else:
                    nc.vector.tensor_tensor(neg_parts[:, :, 3], neg_rest[:, :], neg_parts[:, :, 2],
                                            ALU.subtract).then_inc(max_parts, 1)

            def split_weights():
                dve.wait_ge(taken["W"], 2)
                for i in range(DC):
                    nc.vector.tensor_tensor(by_dimension(w_lo[:, 0, i]), by_head(0, i),
                                            by_dimension(w_hi[:, 0, i].bitcast(F32)), ALU.subtract)\
                        .then_inc(w_low, 1)
                dve.wait_ge(taken["W"], 3)
                nc.vector.tensor_tensor(w_lo[:, 1].rearrange("p i o -> p (i o)"), weight_bank(1),
                                        w_hi[:, 1].rearrange("p i o -> p (i o)").bitcast(F32),
                                        ALU.subtract).then_inc(w_low, 1)

            def take(kind, index, n, at):
                side = side_bank(at, n)
                if kind == "K":
                    dve.wait_ge(k_high, PER["K"] * n + index + 1)
                    wait(dve, k_split, PER["K"] * n + index + 1 - RESID)
                    half, piece = divmod(index, PIECES)
                    lo, hi = CUTS[piece], CUTS[piece + 1]
                    nc.vector.tensor_tensor(k_rest[:, index % RESID, 0:hi - lo], side[:, 0:hi - lo],
                                            k_parts[:, half, 0, lo:hi], ALU.subtract).then_inc(taken["K"], 1)
                    if as_int(n) == 0 and half == 0:
                        dve.wait_ge(taken["K"], index + 1)
                        split_k(dve, nc.vector, 0, index)
                elif kind == "QP":
                    dve.wait_ge(q_high, n + 1)
                    nc.vector.scalar_tensor_tensor(q_rest[:, :], side[:, :], SCALE, q_parts[:, 0, :],
                                                   ALU.mult, ALU.subtract).then_inc(taken["QP"], 1)
                    if as_int(n) == 0:
                        dve.wait_ge(taken["QP"], 1)
                        split_q(dve, nc.vector, 0)
                elif kind == "O":
                    quad = QUADS * n + index
                    dve.wait_ge(full["O"], quad + 1)
                    sums = side[:, 0:TC * P].rearrange("p (c j e) -> p c j e", c=TC, j=QUAD)
                    nc.vector.reciprocal(inv_sum[:, :, :], sums[:, :, :, HD]).then_inc(inverted, 1)
                    dve.wait_ge(inverted, quad + 1)
                    width = QUAD * HD
                    nc.vector.tensor_tensor(
                        attn[:, :, width * index:width * (index + 1)].rearrange("p c (j d) -> p c j d", j=QUAD),
                        sums[:, :, :, 0:HD],
                        inv_sum[:, :, :].unsqueeze(3).broadcast_to([P, TC, QUAD, HD]),
                        ALU.mult).then_inc(taken["O"], 1)
                elif kind == "F":
                    dve.wait_ge(full["F"], n + 1)
                    dve.wait_ge(residual_in, DMA * (n + 1))
                    if as_int(n) == 0:
                        dve.wait_ge(gate_ready, 1)
                    wait(dve, stored, DMA * n)
                    nc.vector.scalar_tensor_tensor(
                        result[:, :, :].rearrange("p c d -> p (c d)"), side[:, :], tanh_gate[:, 0:1],
                        residual[:, :, :].rearrange("p c d -> p (c d)"), ALU.mult, ALU.add)\
                        .then_inc(taken["F"], 1)

            def statistics(n, c):
                if c % 4 == 0:
                    dve.wait_ge(audio_in[c // 4], DMA * (n + 1))
                rows = P if c < SC - 1 else SLAST
                nc.vector.bn_stats(bn[0:rows, c, :], audio[0:rows, c, :]).then_inc(stats, 1)

            def aggregate(n, c):
                rows = P if c < SC - 1 else SLAST
                dve.wait_ge(stats, SC * n + c + 1)
                own_instruction(dve)
                nc.vector.bn_aggr(mean_var[0:rows, c, :], bn[0:rows, c, :]).then_inc(moments, 1)

            def add_eps(n):
                dve.wait_ge(moments, SC * (n + 1))
                nc.vector.tensor_scalar(var_eps[:, :], mean_var[:, :, 1], EPS, None, ALU.add)\
                    .then_inc(eps_added, 1)

            def normalise_own(n, c):
                if c == NORMS["DVE"][0]:
                    dve.wait_ge(rstd_ready, n + 1)
                normalise(nc.vector, "DVE", c)
                if as_int(n) == 0 and c + 1 in NORMS["Pool"]:
                    normalise(nc.vector, "Pool", c + 1)

            def refine(n, link):
                y, t = rstd0[:, :], [newton[:, i, :] for i in range(3)]
                if link == 0:
                    dve.wait_ge(powered, n + 1)
                    nc.vector.tensor_tensor(t[0], y, y, ALU.mult).then_inc(newton_chain, 1)
                    return
                dve.wait_ge(newton_chain, 3 * n + link)
                if link == 1:
                    nc.vector.tensor_tensor(t[1], t[0], var_eps[:, :], ALU.mult).then_inc(newton_chain, 1)
                elif link == 2:
                    nc.vector.tensor_scalar(t[2], t[1], -0.5, 1.5, ALU.mult, ALU.add).then_inc(newton_chain, 1)
                else:
                    nc.vector.tensor_tensor(rstd[:, :], y, t[2], ALU.mult).then_inc(rstd_ready, 1)

            def normalisation(b, k):
                n = b + 1
                if not exists(n):
                    return []
                pieces = []
                if k == 0:
                    wait(dve, normed["Pool"], len(NORMS["Pool"]) * n)
                pieces += [lambda c=c: statistics(n, c) for c in STATS_AT.get(k, ())]
                pieces += [lambda c=c: aggregate(n, c) for c in STATS_AT.get(k - 1, ())]
                if k == EPS_STEP:
                    pieces.append(lambda: add_eps(n))
                if k in (REFINE_STEP, REFINE_STEP + 1):
                    pieces += [lambda i=i: refine(n, 2 * (k - REFINE_STEP) + i) for i in range(2)]
                first = 2 * (k - REFINE_STEP - 2)
                if first >= 0:
                    pieces += [lambda c=c: normalise_own(n, c) for c in NORMS["DVE"][first:first + 2]]
                return pieces

            def body(b):
                for k in range(STEPS):
                    if as_int(b) == -1 and k == REFINE_STEP:
                        split_weights()
                    pieces = normalisation(b, k)
                    for nb, nq, n, at in searches(b, k):
                        search(nb, nq, n, at)
                        if n == FINDS - 1:
                            split_max(nb, nq, 0)
                        elif n < LINKS - 1 and (as_int(nb) > 0 or nq > 0):
                            split_max(nb - (nq == 0), (nq - 1) % QUADS, n + 1)
                        if pieces:
                            pieces.pop(0)()
                    if as_int(b) == -1:
                        for s, kind, index, _ in UNITS:
                            if kind == "XT" and k == max(s + 1, AUDIO_SPLIT_STEP):
                                dve.wait_ge(taken["XT"], index + 1)
                                split_audio(nc.vector, index)
                    if as_int(b) == B - 1 and k == LAST_SEARCH:
                        for link in range(1, LINKS):
                            split_max(b, QUADS - 1, link)
                    for unit in side_units(b, k):
                        take(*unit)
                    if k % SC == 0:
                        quad = QUADS * b + k // SC - 1
                        if exists(b - 1) if k == 0 else exists(b):
                            dve.wait_ge(mixed_done, STEPS * b + k)
                            wait(dve, full["O"], quad)
                            nc.vector.tensor_copy(mixed_sb[:, :], mixed[:, 0:T]).then_inc(mixed_taken, 1)
                    for piece in pieces:
                        piece()

            run_batches(dve, body)

        @block.gpsimd
        def _(pool):
            nc.gpsimd.memset(ident[:, :], 0.0).then_inc(ident0, 1)
            pool.wait_ge(ident0, 1)
            nc.gpsimd.affine_select(out=ident[:, :], in_=ident[:, :], compare_op=ALU.not_equal, fill=1.0,
                                    base=0, pattern=[[-1, P]], channel_multiplier=1).then_inc(ident_ready, 1)
            pool.wait_ge(ident_ready, 1)
            nc.gpsimd.memset(k_rows[0:ROWS, :, S:SPAD], 0.0).then_inc(pool_ready, 1)
            pool.wait_ge(pool_ready, 1)
            two_ones = struct.unpack("<f", struct.pack("<I", 0x3F803F80))[0]
            rows = q_rows[MASK_ROW:ALL_ROWS, :, :].rearrange("p h t -> p (h t)")
            nc.gpsimd.memset(rows.bitcast(F32), two_ones).then_inc(pool_ready, 1)
            pool.wait_ge(pool_ready, 2)

            def ones_of_k(q):
                rows = k_rows[MASK_ROW:ALL_ROWS, QUAD * q:QUAD * (q + 1), :].rearrange("p h s -> p (h s)")
                nc.gpsimd.memset(rows.bitcast(F32), two_ones).then_inc(ones_ready, 1)
                pool.wait_ge(ones_ready, q + 1)

            ones_of_k(0)

            def mask_columns(n, index):
                chunks = [c for c in (2 * index, 2 * index + 1) if c < SC]
                if index == 0:
                    pool.wait_ge(mask_col, n + 1)
                wait(pool, mixed_done, STEPS * (n - 1) + SC * (QUADS - 1) + chunks[-1] + 1)
                own_instruction(pool)
                lo, hi = chunks[0], chunks[-1] + 1
                nc.gpsimd.tensor_copy(v_rows[:, lo:hi, :, HD],
                                      mask_c[:, lo:hi].unsqueeze(2).broadcast_to([P, hi - lo, HEADS]))\
                    .then_inc(v_mask, 1)

            def body(b):
                if exists(b):
                    mask_columns(b, PER["V"] - 1)
                if not exists(b + 1):
                    return
                n = b + 1
                pool.wait_ge(eps_added, n + 1)
                nc.gpsimd.tensor_tensor(rstd0[:, :], var_eps[:, :], minus_half[:, :], ALU.pow)\
                    .then_inc(powered, 1)
                if as_int(b) >= 0:
                    pool.wait_ge(taken["QP"], n + 1)
                    own_instruction(pool)
                    split_q(pool, nc.gpsimd, n)
                    pool.wait_ge(rstd_ready, n + 1)
                    own_instruction(pool)
                    for c in NORMS["Pool"]:
                        normalise(nc.gpsimd, "Pool", c)
                if as_int(b) == -1:
                    pool.wait_ge(normed["Pool"], len(NORMS["Pool"]))
                    for q in range(1, QUADS):
                        ones_of_k(q)
                    pool.wait_ge(taken["MT"], 1)
                wait(pool, taken["V"], PER["V"] * n)
                wait(pool, v_mask, PER["V"] * n)
                own_instruction(pool)
                nc.gpsimd.tensor_copy(mask_c[:, :], mask_t[:, :, bass.ds(n, 1)].rearrange("p c b -> p (c b)"))\
                    .then_inc(mask_col, 1)
                for _, kind, u, _ in UNITS:
                    if kind == "XT" and as_int(b) >= 0:
                        pool.wait_ge(taken["XT"], PER["XT"] * n + u + 1)
                        own_instruction(pool)
                        split_audio(nc.gpsimd, u)
                    if kind == "K" and (as_int(b) >= 0 or u >= PIECES):
                        if as_int(b) == -1 and u == PIECES:
                            pool.wait_ge(k_split, PIECES)
                        pool.wait_ge(taken["K"], PER["K"] * n + u + 1)
                        own_instruction(pool)
                        split_k(pool, nc.gpsimd, n, u)
                for index in range(PER["V"] - 1):
                    mask_columns(n, index)

            run_batches(pool, body)


_INS = ["x", "ctx_2048", "mask_BxS2_bf1", "L0_xattn_Wq", "L0_xattn_Wk", "L0_xattn_Wv", "L0_xattn_Wo",
        "L0_xattn_ln_gamma", "L0_xattn_ln_beta", "L0_xattn_gate"]


def kernel(**inputs):
    import concourse.bacc as bacc
    from concourse.bass_utils import run_bass_kernel_spmd

    nc = bacc.Bacc("TRN2", target_bir_lowering=False, num_devices=1)
    arrays, args = {}, []
    for name in _INS:
        a = np.ascontiguousarray(inputs[name])
        arrays[f"in_{name}"] = a
        args.append(nc.dram_tensor(f"in_{name}", a.shape, mybir.dt.from_np(a.dtype), kind="ExternalInput").ap())
    out = nc.dram_tensor("out_dram", (B, T, D), F32, kind="ExternalOutput").ap()
    xattn_kernel(nc, *args, out)
    r = run_bass_kernel_spmd(nc, [arrays], core_ids=[0])
    return r.results[0]["out_dram"]
```
